# Optimizing a Trainium2 kernel written in Bass

```python
import numpy as np
import jax
import jax.numpy as jnp

def _softmax(x, axis=-1):
    return jax.nn.softmax(x, axis=axis)

def _gelu(x):
    return jax.nn.gelu(x, approximate=True)

def _silu(x):
    return jax.nn.silu(x)

def _sigmoid(x):
    return jax.nn.sigmoid(x)

def _layernorm(x, axis=-1, eps=1e-05):
    m = jnp.mean(x, axis=axis, keepdims=True)
    v = jnp.var(x, axis=axis, keepdims=True)
    return (x - m) / jnp.sqrt(v + eps)

def _scatter_add(tgt, idx, src, axis=0):
    return tgt.at[idx].add(src)

def _segment_sum(src, seg, n):
    return jax.ops.segment_sum(src, seg, n)
kernel_name = 'mk_flamingo_gated_d1_seqx_r4_b3d528'

def setup_inputs(seed: int=0):
    np.random.seed(seed)
    _w = jnp.asarray

    def _rec_inputs():
        import jax
        import jax.numpy as jnp
        _rk = jax.random.key(seed)
        x = -0.0005207 + 1.001 * jax.random.normal(jax.random.fold_in(_rk, 1), (4, 512, 256), jnp.float32)
        _lenS = 512 - jax.random.randint(jax.random.fold_in(_rk, 7), (4,), 0, max(1, 512 // 4) + 1, jnp.int32)
        _lenS2 = 512 - jax.random.randint(jax.random.fold_in(_rk, 8), (4,), 0, max(1, 512 // 4) + 1, jnp.int32)
        _ctx_1024P = jax.random.normal(jax.random.fold_in(_rk, 11), (4, 16, 256), jnp.float32)
        _ctx_1024c = jax.random.dirichlet(jax.random.fold_in(_rk, 511), 0.3 * jnp.ones((16,), jnp.float32), (4, 512))
        _ctx_1024t = jnp.einsum('bsk,bkd->bsd', _ctx_1024c, _ctx_1024P)
        _ctx_1024t = _ctx_1024t * jax.lax.rsqrt(jnp.mean(jnp.square(_ctx_1024t)) + 1e-12) * 0.953939
        ctx_1024 = -1.39393e-06 + 0.999914 * (_ctx_1024t + 0.3 * jax.random.normal(jax.random.fold_in(_rk, 611), (4, 512, 256), jnp.float32))
        _g = jax.random.normal(jax.random.fold_in(_rk, 9001), (2, 1), jnp.float32)
        _g = jnp.sign(_g) * jnp.maximum(jnp.abs(_g), 1.0) + (_g == 0) * 1.0
        g_xattn = _g[0]
        g_ffn = _g[1]
        return (x, ctx_1024, g_xattn, g_ffn)
    x, ctx_1024, g_xattn, g_ffn = _rec_inputs()

    def _L0_xattn_setup():
        import jax, jax.numpy as jnp
        import numpy as np
        DIM = 256
        HEADS = 16
        HEAD_DIM = DIM // HEADS
        SCALE = HEAD_DIM ** (-0.5)
        key = jax.random.key(seed)
        ks = jax.random.split(key, 6)
        B, Nq, Nkv = (2, 256, 512)
        s = DIM ** (-0.5)
        return {'x': jax.random.normal(ks[0], (B, Nq, DIM), jnp.float32), 'mem': jax.random.normal(ks[1], (B, Nkv, DIM), jnp.float32), 'W_kv': jax.random.normal(ks[2], (DIM, 2 * DIM), jnp.float32) * s, 'W_q': jax.random.normal(ks[3], (DIM, DIM), jnp.float32) * s, 'W_proj': jax.random.normal(ks[4], (DIM, DIM), jnp.float32) * s, 'b_proj': jax.random.normal(ks[5], (DIM,), jnp.float32) * 0.01}
    _L0_xattn_all = _L0_xattn_setup()
    _L0_xattn_in = {k: v for k, v in _L0_xattn_all.items() if k in ('W_kv', 'W_q', 'W_proj', 'b_proj')}
    del _L0_xattn_all

    def _L0_ffn_setup():
        import jax, jax.numpy as jnp
        import numpy as np
        B, T, D = (4, 1024, 256)
        E = 8
        TOP_K = 2
        FFN = 768
        HALF = FFN // 2

        def _kaiming_uniform(key, shape, fan_in):
            bound = 1.0 / np.sqrt(fan_in)
            return jax.random.uniform(key, shape, jnp.float32, -bound, bound)
        key = jax.random.key(seed)
        ks = jax.random.split(key, 7)
        x = jax.random.normal(ks[0], (B, T, D), jnp.float32)
        gate_w = _kaiming_uniform(ks[1], (E, D), D) * 0.01
        w_up = _kaiming_uniform(ks[2], (E, FFN, D), D)
        w_down = _kaiming_uniform(ks[3], (E, D, HALF), HALF)
        sg_gate = _kaiming_uniform(ks[4], (HALF, D), D)
        sg_up = _kaiming_uniform(ks[5], (HALF, D), D)
        sg_down = _kaiming_uniform(ks[6], (D, HALF), HALF)
        return {'x': x, 'gate_w': gate_w, 'w_up': w_up, 'w_down': w_down, 'sg_gate': sg_gate, 'sg_up': sg_up, 'sg_down': sg_down}
    _L0_ffn_all = _L0_ffn_setup()
    _L0_ffn_in = {k: v for k, v in _L0_ffn_all.items() if k in ('gate_w', 'w_up', 'w_down', 'sg_gate', 'sg_up', 'sg_down')}
    del _L0_ffn_all
    return {'x': x, 'ctx_1024': ctx_1024, 'g_xattn': g_xattn, 'g_ffn': g_ffn, 'L0_xattn_W_kv': _L0_xattn_in['W_kv'], 'L0_xattn_W_q': _L0_xattn_in['W_q'], 'L0_xattn_W_proj': _L0_xattn_in['W_proj'], 'L0_xattn_b_proj': _L0_xattn_in['b_proj'], 'L0_ffn_gate_w': _L0_ffn_in['gate_w'], 'L0_ffn_w_up': _L0_ffn_in['w_up'], 'L0_ffn_w_down': _L0_ffn_in['w_down'], 'L0_ffn_sg_gate': _L0_ffn_in['sg_gate'], 'L0_ffn_sg_up': _L0_ffn_in['sg_up'], 'L0_ffn_sg_down': _L0_ffn_in['sg_down']}

def reference(x, ctx_1024, g_xattn, g_ffn, L0_xattn_W_kv, L0_xattn_W_q, L0_xattn_W_proj, L0_xattn_b_proj, L0_ffn_gate_w, L0_ffn_w_up, L0_ffn_w_down, L0_ffn_sg_gate, L0_ffn_sg_up, L0_ffn_sg_down):
    import jax
    import jax.numpy as jnp

    def _L0_xattn_ref(x, mem, W_kv, W_q, W_proj, b_proj):
        import jax, jax.numpy as jnp
        import numpy as np
        DIM = 256
        HEADS = 16
        HEAD_DIM = DIM // HEADS
        SCALE = HEAD_DIM ** (-0.5)
        B, Nkv, C = mem.shape
        Nq = x.shape[1]
        kv = (mem @ W_kv).reshape(B, Nkv, 2, HEADS, HEAD_DIM)
        k = kv[:, :, 0].transpose(0, 2, 1, 3)
        v = kv[:, :, 1].transpose(0, 2, 1, 3)
        q = (x @ W_q).reshape(B, Nq, HEADS, HEAD_DIM).transpose(0, 2, 1, 3)
        attn = jnp.einsum('bhqd,bhkd->bhqk', q, k) * SCALE
        attn = jax.nn.softmax(attn, axis=-1)
        out = jnp.einsum('bhqk,bhkd->bhqd', attn, v)
        out = out.transpose(0, 2, 1, 3).reshape(B, Nq, C)
        return out @ W_proj + b_proj

    def _L0_ffn_ref(x, gate_w, w_up, w_down, sg_gate, sg_up, sg_down):
        import jax, jax.numpy as jnp
        import numpy as np
        B, T, D = (4, 1024, 256)
        E = 8
        TOP_K = 2
        FFN = 768
        HALF = FFN // 2

        def _kaiming_uniform(key, shape, fan_in):
            bound = 1.0 / np.sqrt(fan_in)
            return jax.random.uniform(key, shape, jnp.float32, -bound, bound)
        b, t, d = x.shape
        xf = x.reshape(b * t, d)
        N = xf.shape[0]
        logits = xf @ gate_w.T
        topk_logits, topk_idx = jax.lax.top_k(logits, TOP_K)
        topk_w = jax.nn.softmax(topk_logits.astype(jnp.float32), axis=-1).astype(x.dtype)
        comb = jnp.zeros((N, E), x.dtype).at[jnp.arange(N)[:, None], topk_idx].add(topk_w)
        wg = w_up[:, :HALF, :]
        wu = w_up[:, HALF:, :]
        out = jnp.zeros_like(xf)
        for e in range(E):
            g = xf @ wg[e].T
            u = xf @ wu[e].T
            y = jax.nn.silu(g) * u @ w_down[e].T
            out = out + comb[:, e:e + 1] * y
        shared = jax.nn.silu(xf @ sg_gate.T) * (xf @ sg_up.T) @ sg_down.T
        return (shared + out).reshape(b, t, d)
    x = x + jnp.tanh(g_xattn[0]) * _L0_xattn_ref(_layernorm(x, axis=-1), ctx_1024, L0_xattn_W_kv, L0_xattn_W_q, L0_xattn_W_proj, L0_xattn_b_proj)
    x = x + jnp.tanh(g_ffn[0]) * _L0_ffn_ref(_layernorm(x, axis=-1), L0_ffn_gate_w, L0_ffn_w_up, L0_ffn_w_down, L0_ffn_sg_gate, L0_ffn_sg_up, L0_ffn_sg_down)
    return x

_drawn_inputs = setup_inputs


def setup_inputs(seed=0):
    import zlib

    import numpy as np

    out = dict(_drawn_inputs(seed))
    spreads = {}
    factors = {'L0_xattn_b_proj': 6.161}
    for name, (base, spread) in spreads.items():
        noise = np.random.default_rng([zlib.crc32(name.encode()), seed]).standard_normal(out[name].shape)
        drawn = base * np.exp(spread * noise) if base else spread * noise
        out[name] = jnp.asarray(drawn.astype(out[name].dtype))
    for name, factor in factors.items():
        out[name] = (out[name] * factor).astype(out[name].dtype)
    return out
```

```python
from contextlib import ExitStack

import concourse.bass as bass
import numpy as np
from concourse import mybir

P = 128
F32, BF16, I32, U32 = mybir.dt.float32, mybir.dt.bfloat16, mybir.dt.int32, mybir.dt.uint32
ALU = mybir.AluOpType
ACT = mybir.ActivationFunctionType
AX = mybir.AxisListType

B, T, D = 4, 512, 256
N = B * T
NT = N // P
TB = T // P
DC = D // P
H, HD = 16, 16
HG = 4
NG = H // HG
UNITS = B * NG
VW = 32
E, HALF, FFN = 8, 384, 768
FC = HALF // P
TOPK = 2
MAX_BLOCKS = (TOPK * N + E * (P - 1)) // P
EPS = 1e-5
K_PARTS = (0, 1, 2, 0, 1, 0)
Q_PARTS = (0, 0, 0, 1, 1, 2)
KROWS = len(K_PARTS) * HD
MROWS = 3
LOADS = len(K_PARTS) + len(Q_PARTS) + 1


def build(nc, x, ctxT, g_xattn, g_ffn, w_kv, w_q, w_proj, b_proj, gateT, w_upT, w_downT, out):
    qk_parts = nc.dram_tensor("qk_parts", (2, 3, D, N), BF16, kind="Internal").ap()
    v_rows = nc.dram_tensor("v_rows", (B, P, TB, H * VW), F32, kind="Internal").ap()
    x_slots = nc.dram_tensor("x_slots", (MAX_BLOCKS * P, D), F32, kind="Internal").ap()
    y_slots = nc.dram_tensor("y_slots", (MAX_BLOCKS * P, D), F32, kind="Internal").ap()

    x_dram = x.rearrange("b (t p) d -> p (b t) d", p=P)
    out_dram = out.rearrange("b (t p) d -> p (b t) d", p=P)

    with ExitStack() as ctx:
        def sb(name, shape, dt=F32):
            return ctx.enter_context(nc.sbuf_tensor(name, shape, dt))

        def sem(name):
            return ctx.enter_context(nc.semaphore(name))

        x_sb = sb("x_sb", [P, NT, D])
        rows = sb("rows", [P, NT, D])
        xnT = sb("xnT", [P, DC, N])
        ctx_region = sb("ctx_region", [P, DC * N])
        ctx_sb = ctx_region[:, :].rearrange("p (c n) -> p c n", c=DC)
        probs = ctx_region[:, :].rearrange("p (s n) -> p s n", n=T)
        up_region = sb("up_region", [P, (E + 1) * DC * FFN])
        w_up = up_region[:, :].rearrange("p (e c f) -> p e c f", e=E + 1, c=DC)
        w_dn = sb("w_dn", [P, E + 1, FC, D])
        o = 0
        parts = up_region[:, o:o + 2 * 2 * 3 * DC * T // 2].bitcast(BF16).rearrange(
            "p (s a j c n) -> p s a j c n", s=2, a=2, j=3, c=DC)
        o += 2 * 2 * 3 * DC * T // 2
        resid = up_region[:, o:o + 2 * DC * T].rearrange("p (a c n) -> p a c n", a=2, c=DC)
        o += 2 * DC * T
        v_sb = up_region[:, o:o + 2 * TB * H * VW].rearrange("p (s k h w) -> p s k h w", s=2, k=TB, h=H)
        assert o + 2 * TB * H * VW <= (E + 1) * DC * FFN
        unit_words = 2 * 4 * HG * T // 2 + 4 * TB * HG * VW
        unit_region = sb("unit_region", [P, unit_words])
        k_unit = unit_region[:, 0:4 * HG * T // 2].bitcast(BF16).rearrange("p (s h n) -> p s h n", s=4, h=HG)
        q_unit = unit_region[:, 4 * HG * T // 2:4 * HG * T].bitcast(BF16).rearrange(
            "p (s h n) -> p s h n", s=4, h=HG)
        v_unit = unit_region[:, 4 * HG * T:unit_words].rearrange("p (s k c) -> p s k c", s=4, k=TB)
        used = [0]

        def work(words, pattern, **sizes):
            a = used[0]
            used[0] += words
            assert used[0] <= unit_words
            return unit_region[:, a:a + words].rearrange(pattern, **sizes)

        sh_gate = work(FC * T, "p (f n) -> p f n", f=FC)
        sh_hT = work(FC * T, "p (f n) -> p f n", f=FC)
        blk_x = work(2 * D, "p (s d) -> p s d", s=2)
        blk_xT = work(2 * D, "p (s c n) -> p s c n", s=2, c=DC)
        blk_gate = work(HALF, "p f -> p f")
        blk_h = work(HALF, "p f -> p f")
        blk_hT = work(HALF, "p (f n) -> p f n", f=FC)
        blk_y = work(2 * D, "p (s d) -> p s d", s=2)
        attnT = work(2 * D, "p (s c n) -> p s c n", s=2, c=DC)
        logits = work(NT * E, "p (t e) -> p t e", t=NT)
        top8 = work(NT * 8, "p (t e) -> p t e", t=NT)
        onehot = work(2 * NT * E, "p (k t e) -> p k t e", k=2, t=NT)
        rank = work(NT * E, "p (t e) -> p t e", t=NT)
        past = work(MAX_BLOCKS * E, "p (j e) -> p j e", e=E)
        GB = 3
        got = work(GB * 2 * D, "p (s k d) -> p s k d", s=GB, k=2)

        wq_sb = sb("wq_sb", [P, DC, D])
        wkv_sb = sb("wkv_sb", [P, DC, 2 * D])
        wp_sb = sb("wp_sb", [P, DC, D])
        gate_sb = sb("gate_sb", [P, DC, E])
        bias_sb = sb("bias_sb", [P, D])
        gates = sb("gates", [P, 2])
        tanh_g = sb("tanh_g", [P, 2])
        eps_sb = sb("eps_sb", [P, 1])
        ident = sb("ident", [P, P])
        stats = sb("stats", [P, NT, 6])
        mean_var = sb("mean_var", [P, NT, 2])
        std = sb("std", [P, NT])
        rstd = sb("rstd", [P, NT])
        neg_max = sb("neg_max", [P, 2, P])
        nmT = sb("nmT", [HG * TB, P])
        nm_res = sb("nm_res", [HG * TB, P])
        nm_parts = sb("nm_parts", [HG * TB, 3, P], BF16)
        o_sb = sb("o_sb", [P, 2, T])
        rinv = sb("rinv", [P, TB, HG])
        zeros = sb("zeros", [P, D])
        ones_bf = sb("ones_bf", [P, P], BF16)
        before = sb("before", [P, P], BF16)
        before_tile = sb("before_tile", [P, NT, E], BF16)
        same_e = sb("same_e", [P, E])
        same_e_bf = sb("same_e_bf", [P, E], BF16)
        iota_e = sb("iota_e", [P, E])
        iota_b = sb("iota_b", [P, MAX_BLOCKS])
        top8_idx = sb("top8_idx", [P, NT, 8], U32)
        topi = sb("topi", [P, 2, NT])
        chosen = sb("chosen", [P, NT, E], BF16)
        totals = sb("totals", [P, P], BF16)
        count = sb("count", [P, E])
        count_i = sb("count_i", [P, E], I32)
        blocks_i = sb("blocks_i", [P, E], I32)
        blocks = sb("blocks", [P, E])
        ends = sb("ends", [P, E])
        base = sb("base", [P, E])
        block_e = sb("block_e", [P, MAX_BLOCKS])
        block_ei = sb("block_ei", [P, MAX_BLOCKS], I32)
        slot_f = sb("slot_f", [P, 2, NT])
        slot_i = sb("slot_i", [P, 2, NT], I32)
        pexp = sb("pexp", [P, 2, NT])
        wsel = sb("wsel", [P, 2, NT])

        ps = [ctx.enter_context(nc.psum_tensor(f"ps{i}", [P, 4, 512], F32)) for i in range(2)]

        def bank(i, n=1):
            return ps[i // 4][:, i % 4, :] if n == 1 else ps[i // 4][:, i % 4:i % 4 + n, :]

        x_in = [sem(f"x_in{b}") for b in range(B)]
        ctx_in = [sem(f"ctx_in{b}") for b in range(B)]
        w_attn_in = sem("w_attn_in")
        small_in = sem("small_in")
        const_step = sem("const_step")
        ident_done = sem("ident_done")
        tanh_done = sem("tanh_done")
        bias_done = sem("bias_done")
        ones_rows = sem("ones_rows")
        v_ones = sem("v_ones")
        resid_base = sem("resid_base")
        stat_done = sem("stat_done")
        var_done = sem("var_done")
        std_done = sem("std_done")
        rstd_done = sem("rstd_done")
        rows_done = sem("rows_done")
        rowsT_ps = sem("rowsT_ps")
        rowsT_sb = sem("rowsT_sb")
        k_ps, v_ps, q_ps = sem("k_ps"), sem("v_ps"), sem("q_ps")
        high_done = sem("high_done")
        resid_done = sem("resid_done")
        v_done = sem("v_done")
        mid_done = sem("mid_done")
        low_done = sem("low_done")
        qkv_out = [sem(f"qkv_out{s}") for s in range(2)]
        unit_in = [sem(f"unit_in{s}") for s in range(4)]
        pair_ps = sem("pair_ps")
        max_done = sem("max_done")
        nmT_ps, nmT_sb = sem("nmT_ps"), sem("nmT_sb")
        nm_step = sem("nm_step")
        nm_split = sem("nm_split")
        nm_in = [sem(f"nm_in{s}") for s in range(4)]
        score_ps = sem("score_ps")
        exp_done = sem("exp_done")
        pv_done = sem("pv_done")
        o_done = sem("o_done")
        oT_ps = sem("oT_ps")
        rinv_done = sem("rinv_done")
        attn_rows = sem("attn_rows")
        w_ffn_in = sem("w_ffn_in")
        zero_out = sem("zero_out")
        atT_ps, atT_sb = sem("atT_ps"), sem("atT_sb")
        proj_ps = sem("proj_ps")
        x1_done = sem("x1_done")
        logit_ps = sem("logit_ps")
        route = sem("route")
        chosen_done = sem("chosen_done")
        totals_ps, totals_sb = sem("totals_ps"), sem("totals_sb")
        rank_ps = sem("rank_ps")
        pexp_done = sem("pexp_done")
        slots_done = sem("slots_done")
        wsel_done = sem("wsel_done")
        scattered = sem("scattered")
        sh_up_ps = sem("sh_up_ps")
        sh_silu = sem("sh_silu")
        sh_hid = sem("sh_hid")
        sh_y_ps = sem("sh_y_ps")
        sh_added = sem("sh_added")
        bx_in = [sem(f"bx_in{s}") for s in range(2)]
        bxT_ps, bxT_sb = sem("bxT_ps"), sem("bxT_sb")
        bup_ps = sem("bup_ps")
        bsilu = sem("bsilu")
        bhid = sem("bhid")
        bhT_ps, bhT_sb = sem("bhT_ps"), sem("bhT_sb")
        by_ps, by_sb = sem("by_ps"), sem("by_sb")
        by_out = [sem(f"by_out{s}") for s in range(2)]
        got_in = [sem(f"got_in{s}") for s in range(GB)]
        added = sem("added")
        out_done = sem("out_done")

        block = ctx.enter_context(nc.Block())

        @block.sync
        def _(sp):
            for b in range(B):
                sp.dma_start(x_sb[:, b * TB:(b + 1) * TB, :], x_dram[:, b * TB:(b + 1) * TB, :]).then_inc(x_in[b], 16)
                if b == 0:
                    sp.dma_start(wkv_sb[:, :, :], w_kv.rearrange("(c p) n -> p c n", p=P)).then_inc(w_attn_in, 16)
                    sp.dma_start(wq_sb[:, :, :], w_q.rearrange("(c p) n -> p c n", p=P)).then_inc(w_attn_in, 16)
                sp.dma_start(ctx_sb[:, :, b * T:(b + 1) * T],
                             ctxT.rearrange("(c p) n -> p c n", p=P)[:, :, b * T:(b + 1) * T]).then_inc(ctx_in[b], 16)
            for b in range(B):
                s = b % 2
                for i, a in enumerate((1, 0)):
                    sp.wait_ge(low_done, 2 * b + i + 1)
                    for j in range(3):
                        sp.dma_start(qk_parts[a, j, :, b * T:(b + 1) * T].rearrange("(c p) n -> p c n", p=P),
                                     parts[:, s, a, j, :, :]).then_inc(qkv_out[s], 16)
                sp.wait_ge(v_done, b + 1)
                sp.dma_start(v_rows[b, :, :, :], v_sb[:, s, :, :, :].rearrange("p k h w -> p k (h w)")
                             ).then_inc(qkv_out[s], 16)
            for s in range(2):
                sp.wait_ge(qkv_out[s], 16 * 7 * (B // 2))

            def load_unit(b, g):
                for side, a, dst in ((K_PARTS, 1, k_unit), (Q_PARTS, 0, q_unit)):
                    for r, j in enumerate(side):
                        src = qk_parts[a, j, g * HG * HD:(g + 1) * HG * HD, bass.ds(b * T, T)].rearrange(
                            "(h d) n -> d h n", d=HD)
                        sp.dma_start(dst[r * HD:(r + 1) * HD, g, :, :], src).then_inc(unit_in[g], 16)
                src = v_rows[bass.ds(b, 1), :, :, g * HG * VW:(g + 1) * HG * VW].rearrange("a p k c -> p (a k) c")
                sp.dma_start(v_unit[:, g, :, :], src).then_inc(unit_in[g], 16)

            for g in range(NG):
                load_unit(0, g)
            with sp.Fori(0, B - 1) as b:
                for g in range(NG):
                    sp.wait_ge(pv_done, (b * NG + g) * TB + TB)
                    load_unit(b + 1, g)

            def load_block(j, s):
                sp.dma_start(blk_x[:, s, :], x_slots[bass.ds(j * P, P), :]).then_inc(bx_in[s], 16)

            def store_block(j, s):
                sp.wait_ge(by_sb, j + 1)
                sp.dma_start(y_slots[bass.ds(j * P, P), :], blk_y[:, s, :]).then_inc(by_out[s], 16)

            sp.wait_ge(zero_out, 16)
            sp.wait_ge(scattered, 16 * 2 * NT)
            load_block(0, 0)
            load_block(1, 1)
            for j in (2, 3):
                sp.wait_ge(bxT_ps, j - 1)
                load_block(j, j % 2)

            def sp_block(j, s, load):
                if load:
                    sp.wait_ge(bxT_ps, j + 3)
                    load_block(j + 4, s)
                store_block(j, s)

            sp_block(0, 0, True)
            PAIRS = (MAX_BLOCKS - 5) // 2
            with sp.Fori(0, PAIRS) as i:
                sp_block(i * 2 + 1, 1, True)
                sp_block(i * 2 + 2, 0, True)
            for j in range(1 + 2 * PAIRS, MAX_BLOCKS):
                sp_block(j, j % 2, j + 4 < MAX_BLOCKS)
            for t in range(NT):
                sp.wait_ge(added, t + 1)
                sp.dma_start(out_dram[:, t, :], x_sb[:, t, :]).then_inc(out_done, 16)
            sp.wait_ge(out_done, 16 * NT)

        @block.gpsimd
        def _(pool):
            nc.gpsimd.memset(ident[:, :], 0.0).then_inc(const_step, 1)
            pool.wait_ge(const_step, 1)
            nc.gpsimd.affine_select(out=ident[:, :], in_=ident[:, :], compare_op=ALU.not_equal, fill=1.0, base=0,
                                    pattern=[[-1, P]], channel_multiplier=1).then_inc(ident_done, 1)
            pool.wait_ge(ident_done, 1)
            nc.gpsimd.memset(zeros[:, :], 0.0).then_inc(const_step, 1)
            pool.wait_ge(const_step, 2)
            nc.gpsimd.memset(neg_max[:, :, :], 0.0).then_inc(const_step, 1)
            pool.wait_ge(const_step, 3)
            nc.gpsimd.memset(ones_bf[:, :], 1.0).then_inc(const_step, 1)
            pool.wait_ge(const_step, 4)
            nc.gpsimd.affine_select(out=before[:, :], in_=ones_bf[:, :], compare_op=ALU.is_gt, fill=0.0, base=0,
                                    pattern=[[1, P]], channel_multiplier=-1).then_inc(const_step, 1)
            pool.wait_ge(const_step, 5)
            nc.gpsimd.iota(iota_e[:, :], pattern=[[1, E]], base=0, channel_multiplier=0,
                           allow_small_or_imprecise_dtypes=True).then_inc(const_step, 1)
            pool.wait_ge(const_step, 6)
            nc.gpsimd.iota(iota_b[:, :], pattern=[[1, MAX_BLOCKS]], base=0, channel_multiplier=0,
                           allow_small_or_imprecise_dtypes=True).then_inc(const_step, 1)
            pool.wait_ge(const_step, 7)
            nc.gpsimd.memset(v_sb[:, :, :, :, HD:VW], 1.0).then_inc(v_ones, 1)
            pool.wait_ge(v_ones, 1)
            nc.gpsimd.memset(k_unit[KROWS:KROWS + MROWS, :, :, :], 1.0).then_inc(ones_rows, 1)
            pool.wait_ge(ones_rows, 1)
            n = 0
            for b in range(B):
                for a in (1, 0):
                    s = b % 2
                    n += 1
                    pool.wait_ge(resid_done, n)
                    nc.gpsimd.tensor_copy(parts[:, s, a, 1, :, :], resid[:, a, :, :]).then_inc(mid_done, 1)
                    pool.wait_ge(mid_done, n)
                    nc.gpsimd.tensor_tensor(parts[:, s, a, 2, :, :], resid[:, a, :, :], parts[:, s, a, 1, :, :],
                                            ALU.subtract).then_inc(low_done, 1)
                    pool.wait_ge(low_done, n)
            pool.wait_ge(route, 2)
            nc.gpsimd.affine_select(out=before_tile[:, :, :], in_=before_tile[:, :, :], compare_op=ALU.is_gt,
                                    fill=0.0, base=0, pattern=[[E, NT], [1, E]], channel_multiplier=-1
                                    ).then_inc(const_step, 1)
            pool.wait_ge(const_step, 8)
            pool.wait_ge(bias_done, 1)
            for t in range(NT):
                pool.wait_ge(rows_done, t // TB + 1)
                nc.gpsimd.tensor_tensor(x_sb[:, t, :], x_sb[:, t, :], bias_sb[:, :], ALU.add).then_inc(resid_base, 1)
            pool.wait_ge(resid_base, NT)

            def split_max(u, b, g):
                pool.wait_ge(nmT_sb, u + 1)
                nc.gpsimd.tensor_copy(nm_parts[:, 0, :], nmT[:, :]).then_inc(nm_step, 1)
                pool.wait_ge(nm_step, 3 * u + 1)
                nc.gpsimd.tensor_tensor(nm_res[:, :], nmT[:, :], nm_parts[:, 0, :], ALU.subtract).then_inc(nm_step, 1)
                pool.wait_ge(nm_step, 3 * u + 2)
                nc.gpsimd.tensor_copy(nm_parts[:, 1, :], nm_res[:, :]).then_inc(nm_step, 1)
                pool.wait_ge(nm_step, 3 * u + 3)
                nc.gpsimd.tensor_tensor(nm_parts[:, 2, :], nm_res[:, :], nm_parts[:, 1, :], ALU.subtract
                                        ).then_inc(nm_split, 1)
                pool.wait_ge(nm_split, u + 1)
                for j in range(MROWS):
                    dst = q_unit[KROWS + j:KROWS + j + 1, g, :, :].rearrange("a h (t n) -> a (h t) n", n=P)
                    pool.dma_start(dst, nm_parts[:, j, :]).then_inc(nm_in[g], 16)
                pool.wait_ge(nm_in[g], (b + 1) * 16 * MROWS)

            for u in range(UNITS):
                split_max(u, u // NG, u % NG)

            pool.wait_ge(slots_done, 1)
            pool.wait_ge(zero_out, 16)
            for t in range(NT):
                for k in range(TOPK):
                    pool.indirect_dma_start(
                        out=x_slots[:, :], out_offset=bass.IndirectOffsetOnAxis(ap=slot_i[:, k, t:t + 1], axis=0),
                        in_=rows[:, t, :], in_offset=None).then_inc(scattered, 16)
            for s in range(2):
                pool.wait_ge(by_out[s], 16 * ((MAX_BLOCKS + 1 - s) // 2))
            for t in range(NT):
                if t >= GB:
                    pool.wait_ge(added, t - GB + 1)
                for k in range(TOPK):
                    pool.indirect_dma_start(
                        out=got[:, t % GB, k, :], out_offset=None, in_=y_slots[:, :],
                        in_offset=bass.IndirectOffsetOnAxis(ap=slot_i[:, k, t:t + 1], axis=0)
                        ).then_inc(got_in[t % GB], 16)

        @block.scalar
        def _(act):
            act.dma_start(gates[:, 0:1], g_xattn.partition_broadcast(P)).then_inc(small_in, 16)
            act.dma_start(gates[:, 1:2], g_ffn.partition_broadcast(P)).then_inc(small_in, 16)
            act.dma_start(bias_sb[:, :], b_proj.partition_broadcast(P)).then_inc(small_in, 16)
            act.dma_start(wp_sb[:, :, :], w_proj.rearrange("(c p) n -> p c n", p=P)).then_inc(small_in, 16)
            act.dma_start(gate_sb[:, :, :], gateT.rearrange("(c p) n -> p c n", p=P)).then_inc(small_in, 16)
            act.wait_ge(const_step, 2)
            act.dma_start(x_slots.rearrange("(j p) d -> p j d", p=P),
                          zeros[:, :].unsqueeze(1).to_broadcast([P, MAX_BLOCKS, D])).then_inc(zero_out, 16)
            act.wait_ge(small_in, 16 * 5)
            nc.scalar.activation(tanh_g[:, :], gates[:, :], ACT.Tanh).then_inc(tanh_done, 1)

            def std_of(b, n):
                act.wait_ge(var_done, n)
                nc.scalar.activation(std[:, b * TB:(b + 1) * TB], mean_var[:, b * TB:(b + 1) * TB, 1], ACT.Sqrt,
                                     bias=eps_sb[:, 0:1]).then_inc(std_done, 1)

            act.wait_ge(bias_done, 1)
            for b in range(B):
                std_of(b, b + 1)
            for b in range(B):
                s = b % 2
                act.wait_ge(rowsT_ps, b + 1)
                nc.scalar.copy(xnT[:, :, b * T:(b + 1) * T], bank(0, 2)).then_inc(rowsT_sb, 1)
                if b >= 2:
                    act.wait_ge(qkv_out[s], 16 * 7 * (b // 2))
                act.wait_ge(k_ps, b + 1)
                nc.scalar.copy(parts[:, s, 1, 0, :, :], bank(4, 2)).then_inc(high_done, 1)
                act.wait_ge(v_ps, b + 1)
                if b == 0:
                    act.wait_ge(v_ones, 1)
                nc.scalar.copy(v_sb[:, s, :, :, 0:HD],
                               bank(6, 2).rearrange("p a (k h w) -> p (a k) h w", k=2, h=H)).then_inc(v_done, 1)
                act.wait_ge(q_ps, b + 1)
                nc.scalar.mul(parts[:, s, 0, 0, :, :], bank(2, 2), float(HD) ** -0.5).then_inc(high_done, 1)
            for s in range(2):
                act.wait_ge(qkv_out[s], 16 * 7 * (B // 2))
            for e in (E, *range(E)):
                act.dma_start(w_up[:, e, :, :], w_upT[e, :, :].rearrange("(c p) f -> p c f", p=P)).then_inc(w_ffn_in, 16)
                act.dma_start(w_dn[:, e, :, :], w_downT[e, :, :].rearrange("(c p) n -> p c n", p=P)
                              ).then_inc(w_ffn_in, 16)

            def copy_max(u):
                if not isinstance(u, int) or u >= 1:
                    act.wait_ge(nm_split, u)
                act.wait_ge(nmT_ps, u + 1)
                nc.scalar.copy(nmT[:, :], bank(7)[0:HG * TB, 0:P]).then_inc(nmT_sb, 1)

            def copy_out(u, s):
                act.wait_ge(pv_done, u * TB + TB)
                nc.scalar.copy(o_sb[:, s, :], bank(6)).then_inc(o_done, 1)

            def exp_slot(u, g, first=False, more_max=True):
                for k in range(TB * HG):
                    kt = k // HG
                    if k % HG == 0 and not (first and kt < 2):
                        act.wait_ge(pv_done, u * TB + kt - 1)
                    act.wait_ge(score_ps, u * TB * HG + k + 1)
                    nc.scalar.activation(probs[:, k % 8, :], bank(4 + k % 2), ACT.Exp).then_inc(exp_done, 1)
                    if k == 5 and not first:
                        copy_out(u - 1, (g + 1) % 2)
                    if k == 7 and more_max:
                        copy_max(u + 1)

            copy_max(0)
            exp_slot(0, 0, first=True)
            with act.Fori(0, B - 1) as b:
                for r in range(1, NG + 1):
                    exp_slot(b * NG + r, r % NG)
            for u in range(UNITS - 3, UNITS):
                exp_slot(u, u % NG, more_max=u + 1 < UNITS)
            copy_out(UNITS - 1, (UNITS - 1) % 2)

            for t in range(NT):
                act.wait_ge(atT_ps, t + 1)
                if t >= 2:
                    act.wait_ge(proj_ps, t - 1)
                nc.scalar.copy(attnT[:, t % 2, :, :], bank(t % 2)[:, 0:D].rearrange("p (c n) -> p c n", c=DC)
                               ).then_inc(atT_sb, 1)
            for b in range(B):
                std_of(b, B + b + 1)
                act.wait_ge(rowsT_ps, B + b + 1)
                nc.scalar.copy(xnT[:, :, b * T:(b + 1) * T], bank(4 + 2 * (b % 2), 2)).then_inc(rowsT_sb, 1)
            act.wait_ge(route, 3)
            nc.scalar.activation(pexp[:, 1, :], pexp[:, 0, :], ACT.Exp).then_inc(pexp_done, 1)

            def shared_silu(i, f):
                act.wait_ge(sh_up_ps, FC * i + f + 1)
                if not isinstance(i, int) or i >= 1:
                    act.wait_ge(sh_hid, FC * i + f - FC + 1)
                nc.scalar.activation(sh_gate[:, f, :], bank(f), ACT.Silu).then_inc(sh_silu, 1)

            for f in range(FC):
                shared_silu(0, f)
            with act.Fori(1, B) as i:
                for f in range(FC):
                    shared_silu(i, f)

            def block_silu(j, first=False):
                act.wait_ge(bup_ps, j + 1)
                if not first:
                    act.wait_ge(bhid, j)
                nc.scalar.activation(blk_gate[:, :], blk_gu_bank(j, 0), ACT.Silu).then_inc(bsilu, 1)

            def blk_gu_bank(j, which):
                return bank(2 * par[0] + which)[:, 0:HALF]

            def block_hT(j, first=False):
                act.wait_ge(bhT_ps, j + 1)
                if not first:
                    act.wait_ge(by_ps, j)
                nc.scalar.copy(blk_hT[:, :, :], bank(5)[:, 0:HALF].rearrange("p (f n) -> p f n", f=FC)
                               ).then_inc(bhT_sb, 1)

            par = [0]
            block_silu(0, first=True)
            block_hT(0, first=True)
            par[0] = 1
            block_silu(1)
            with act.Fori(0, (MAX_BLOCKS - 3) // 2) as i:
                for q in range(2):
                    block_hT(i * 2 + 1 + q)
                    par[0] = q
                    block_silu(i * 2 + 2 + q)
            block_hT(MAX_BLOCKS - 2)
            par[0] = (MAX_BLOCKS - 1) % 2
            block_silu(MAX_BLOCKS - 1)
            block_hT(MAX_BLOCKS - 1)

        @block.vector
        def _(dve):
            nc.vector.memset(eps_sb[:, :], EPS)
            dve.sem_inc(attn_rows, 1)
            dve.wait_ge(tanh_done, 1)
            nc.vector.tensor_scalar(bias_sb[:, :], bias_sb[:, :], tanh_g[:, 0:1], None, ALU.mult
                                    ).then_inc(bias_done, 1)

            def ln_stats(b, n):
                for t in range(b * TB, (b + 1) * TB):
                    last = nc.vector.bn_stats(stats[:, t, :], x_sb[:, t, :])
                last.then_inc(stat_done, 1)
                dve.wait_ge(stat_done, n)
                for t in range(b * TB, (b + 1) * TB):
                    last = nc.vector.bn_aggr(mean_var[:, t, :], stats[:, t, :])
                last.then_inc(var_done, 1)

            def ln_apply(b, n):
                dve.wait_ge(std_done, n)
                nc.vector.reciprocal(rstd[:, b * TB:(b + 1) * TB], std[:, b * TB:(b + 1) * TB]).then_inc(rstd_done, 1)
                dve.wait_ge(rstd_done, n)
                for t in range(b * TB, (b + 1) * TB):
                    last = nc.vector.tensor_scalar(rows[:, t, :], x_sb[:, t, :], mean_var[:, t, 0:1],
                                                   rstd[:, t:t + 1], ALU.subtract, ALU.mult)
                last.then_inc(rows_done, 1)

            for b in range(B):
                dve.wait_ge(x_in[b], 16)
                ln_stats(b, b + 1)
            for b in range(B):
                ln_apply(b, b + 1)
            n = 0
            for b in range(B):
                for a, first_bank, scale in ((1, 4, 1.0), (0, 2, float(HD) ** -0.5)):
                    n += 1
                    dve.wait_ge(high_done, n)
                    if n >= 3:
                        dve.wait_ge(low_done, n - 2)
                    for c in range(DC):
                        last = nc.vector.scalar_tensor_tensor(resid[:, a, c, :], bank(first_bank + c), scale,
                                                              parts[:, b % 2, a, 0, c, :], ALU.mult, ALU.subtract)
                    last.then_inc(resid_done, 1)
                if b == 0:
                    dve.wait_ge(ident_done, 1)
                    nc.vector.tensor_reduce(same_e[:, :], ident[:, :].rearrange("p (t e) -> p e t", e=E), AX.X,
                                            ALU.add).then_inc(route, 1)
                    dve.wait_ge(route, 1)
                    nc.vector.tensor_copy(same_e_bf[:, :], same_e[:, :])
                    nc.vector.tensor_copy(before_tile[:, :, :],
                                          same_e[:, :].unsqueeze(1).to_broadcast([P, NT, E])).then_inc(route, 1)

            def max_pair(w, p, s):
                dve.wait_ge(pair_ps, 8 * w + p + 1)
                nc.vector.tensor_reduce(neg_max[:, s, 2 * p:2 * p + 2], bank(2 * (p % 2), 2), AX.X, ALU.max,
                                        negate=True).then_inc(max_done, 1)

            def normalise(u, b, g):
                dve.wait_ge(oT_ps, u + 1)
                o4 = bank(7).rearrange("p (t h w) -> p t h w", t=TB, h=HG)
                nc.vector.reciprocal(rinv[:, :, :], o4[:, :, :, HD]).then_inc(rinv_done, 1)
                dve.wait_ge(rinv_done, u + 1)
                dst = rows[:, bass.ds(b * TB, TB), g * HG * HD:(g + 1) * HG * HD].rearrange(
                    "p t (h w) -> p t h w", h=HG)
                nc.vector.tensor_tensor(dst, o4[:, :, :, 0:HD],
                                        rinv[:, :, :].unsqueeze(3).to_broadcast([P, TB, HG, HD]), ALU.mult
                                        ).then_inc(attn_rows, 1)

            dve.wait_ge(const_step, 3)
            for w in range(2):
                for p in range(8):
                    max_pair(w, p, w)
            for p in range(8):
                max_pair(2, p, 0)

            def dve_slot(u, bu, gu, s, more_max):
                for p in range(8):
                    if more_max:
                        max_pair(u + 2, p, s)
                    if p == 5:
                        normalise(u - 1, bu, gu)

            with dve.Fori(0, B - 1) as b:
                for r in range(1, NG + 1):
                    dve_slot(b * NG + r, b, r - 1, r % 2, True)
            for u in range(UNITS - 3, UNITS + 1):
                dve_slot(u, (u - 1) // NG, (u - 1) % NG, u % 2, u + 2 < UNITS)

            for t in range(NT):
                dve.wait_ge(proj_ps, t + 1)
                if t == 0:
                    dve.wait_ge(resid_base, NT)
                nc.vector.scalar_tensor_tensor(x_sb[:, t, :], bank(2 + t % 2)[:, 0:D], tanh_g[:, 0:1], x_sb[:, t, :],
                                               ALU.mult, ALU.add).then_inc(x1_done, 1)
            for b in range(B):
                dve.wait_ge(x1_done, (b + 1) * TB)
                ln_stats(b, B + b + 1)
            for b in range(B):
                ln_apply(b, B + b + 1)

            r = [2]

            def step(ins):
                r[0] += 1
                ins.then_inc(route, 1)
                dve.wait_ge(route, r[0])

            dve.wait_ge(logit_ps, 1)
            nc.vector.tensor_copy(logits[:, :, :], bank(0)[:, 0:NT * E].rearrange("p (t e) -> p t e", e=E)
                                  ).then_inc(chosen_done, 1)
            dve.wait_ge(chosen_done, 1)
            for t in range(NT):
                last = nc.vector.max(top8[:, t, :], logits[:, t, :])
            last.then_inc(chosen_done, 1)
            dve.wait_ge(chosen_done, 2)
            step(nc.vector.tensor_tensor(pexp[:, 0, :], top8[:, :, 1], top8[:, :, 0], ALU.subtract))
            for t in range(NT):
                last = nc.vector.max_index(top8_idx[:, t, :], top8[:, t, :], logits[:, t, :])
            step(last)
            step(nc.vector.tensor_copy(topi[:, :, :], top8_idx[:, :, 0:2].rearrange("p t k -> p k t")))
            for k in range(TOPK):
                last = nc.vector.tensor_tensor(onehot[:, k, :, :], topi[:, k, :].unsqueeze(2).to_broadcast([P, NT, E]),
                                               iota_e[:, :].unsqueeze(1).to_broadcast([P, NT, E]), ALU.is_equal)
            step(last)
            nc.vector.tensor_tensor(chosen[:, :, :], onehot[:, 0, :, :], onehot[:, 1, :, :], ALU.add
                                    ).then_inc(chosen_done, 1)
            dve.wait_ge(totals_ps, 1)
            nc.vector.tensor_copy(totals[:, :], bank(1)[:, 0:1].to_broadcast([P, P])).then_inc(totals_sb, 1)
            dve.wait_ge(rank_ps, 1)
            nc.vector.tensor_copy(rank[:, :, :], bank(2)[:, 0:NT * E].rearrange("p (t e) -> p t e", e=E))
            step(nc.vector.tensor_copy(count[:, :], bank(3)[:, 0:E]))
            step(nc.vector.tensor_scalar(count_i[:, :], count[:, :], float(P - 1), None, ALU.add))
            step(nc.vector.tensor_scalar(blocks_i[:, :], count_i[:, :], 7, None, ALU.logical_shift_right))
            step(nc.vector.tensor_copy(blocks[:, :], blocks_i[:, :]))
            step(nc.vector.tensor_tensor_scan(ends[:, :], ones_bf[:, 0:E], blocks[:, :], 0.0, ALU.mult, ALU.add))
            step(nc.vector.tensor_tensor(base[:, :], ends[:, :], blocks[:, :], ALU.subtract))
            step(nc.vector.scalar_tensor_tensor(rank[:, :, :], base[:, :].unsqueeze(1).to_broadcast([P, NT, E]),
                                                float(P), rank[:, :, :], ALU.mult, ALU.add))
            step(nc.vector.tensor_tensor(onehot[:, :, :, :], onehot[:, :, :, :],
                                         rank[:, :, :].unsqueeze(1).to_broadcast([P, 2, NT, E]), ALU.mult))
            step(nc.vector.tensor_reduce(slot_f[:, :, :], onehot[:, :, :, :], AX.X, ALU.add))
            nc.vector.tensor_copy(slot_i[:, :, :], slot_f[:, :, :]).then_inc(slots_done, 1)
            step(nc.vector.tensor_tensor(past[:, :, :], ends[:, :].unsqueeze(1).to_broadcast([P, MAX_BLOCKS, E]),
                                         iota_b[:, :].unsqueeze(2).to_broadcast([P, MAX_BLOCKS, E]), ALU.is_le))
            step(nc.vector.tensor_reduce(block_e[:, :], past[:, :, :], AX.X, ALU.add))
            nc.vector.tensor_scalar(block_ei[:, :], block_e[:, :], float(E - 1), None, ALU.min).then_inc(slots_done, 1)
            dve.wait_ge(pexp_done, 1)
            step(nc.vector.tensor_scalar(wsel[:, 1, :], pexp[:, 1, :], 1.0, None, ALU.add))
            step(nc.vector.reciprocal(wsel[:, 0, :], wsel[:, 1, :]))
            step(nc.vector.tensor_scalar(wsel[:, 0, :], wsel[:, 0, :], tanh_g[:, 1:2], None, ALU.mult))
            nc.vector.tensor_tensor(wsel[:, 1, :], wsel[:, 0, :], pexp[:, 1, :], ALU.mult).then_inc(wsel_done, 1)

            def shared_hidden(i, first):
                for f in range(FC):
                    dve.wait_ge(sh_silu, FC * i + f + 1)
                    if not first:
                        dve.wait_ge(sh_y_ps, 2 * i)
                    nc.vector.tensor_tensor(sh_hT[:, f, :], sh_gate[:, f, :], bank(3 + f), ALU.mult
                                            ).then_inc(sh_hid, 1)
                for q in range(2):
                    dve.wait_ge(sh_y_ps, 2 * i + q + 1)
                    dst = x_sb[:, bass.ds(i * TB + 2 * q, 2), :]
                    nc.vector.scalar_tensor_tensor(dst, bank(6 + q).rearrange("p (t d) -> p t d", t=2),
                                                   tanh_g[:, 1:2], dst, ALU.mult, ALU.add).then_inc(sh_added, 1)

            shared_hidden(0, True)
            with dve.Fori(1, B) as i:
                shared_hidden(i, False)

            def copy_xT(j, s, first=False):
                dve.wait_ge(bxT_ps, j + 1)
                if not first:
                    dve.wait_ge(bup_ps, j - 1)
                nc.vector.tensor_copy(blk_xT[:, s, :, :], bank(4)[:, 0:D].rearrange("p (c n) -> p c n", c=DC)
                                      ).then_inc(bxT_sb, 1)

            def hidden(j, s, first=False):
                dve.wait_ge(bsilu, j + 1)
                if not first:
                    dve.wait_ge(bhT_ps, j)
                nc.vector.tensor_tensor(blk_h[:, :], blk_gate[:, :], bank(2 * s + 1)[:, 0:HALF], ALU.mult
                                        ).then_inc(bhid, 1)

            def copy_y(j, s, first=False):
                dve.wait_ge(by_ps, j + 1)
                if not first:
                    dve.wait_ge(by_out[s], ((j - s) // 2 if isinstance(j, int) else j_half[0]) * 16)
                nc.vector.tensor_copy(blk_y[:, s, :], bank(6 + s)[:, 0:D]).then_inc(by_sb, 1)

            j_half = [None]
            copy_xT(0, 0, first=True)
            copy_xT(1, 1, first=True)
            hidden(0, 0, first=True)
            copy_xT(2, 0)
            hidden(1, 1)
            copy_y(0, 0, first=True)
            copy_xT(3, 1)
            hidden(2, 0)
            copy_y(1, 1, first=True)
            with dve.Fori(0, (MAX_BLOCKS - 5) // 2) as i:
                for q in range(2):
                    copy_xT(i * 2 + 4 + q, q)
                    hidden(i * 2 + 3 + q, (1 + q) % 2)
                    j_half[0] = i + 1
                    copy_y(i * 2 + 2 + q, q)
            for j in range(2 + 2 * ((MAX_BLOCKS - 5) // 2), MAX_BLOCKS):
                if j + 2 < MAX_BLOCKS:
                    copy_xT(j + 2, j % 2)
                if j + 1 < MAX_BLOCKS:
                    hidden(j + 1, (j + 1) % 2)
                copy_y(j, j % 2)

            for t in range(NT):
                dve.wait_ge(got_in[t % GB], 16 * TOPK * (t // GB + 1))
                nc.vector.scalar_tensor_tensor(x_sb[:, t, :], got[:, t % GB, 0, :], wsel[:, 0, t:t + 1], x_sb[:, t, :],
                                               ALU.mult, ALU.add).then_inc(x1_done, 1)
                dve.wait_ge(x1_done, NT + t + 1)
                nc.vector.scalar_tensor_tensor(x_sb[:, t, :], got[:, t % GB, 1, :], wsel[:, 1, t:t + 1], x_sb[:, t, :],
                                               ALU.mult, ALU.add).then_inc(added, 1)

        @block.tensor
        def _(pe):
            def mm(o_, w, m, start=True, stop=True):
                return nc.tensor.matmul(o_, w, m, start=start, stop=stop)

            pe.wait_ge(ident_done, 1)
            pe.wait_ge(w_attn_in, 32)
            for b in range(B):
                pe.wait_ge(ctx_in[b], 16)
                if b >= 1:
                    pe.wait_ge(resid_done, 2 * b - 1)
                for c in range(DC):
                    for d in range(DC):
                        last = mm(bank(4 + c), wkv_sb[:, d, c * P:(c + 1) * P], ctx_sb[:, d, b * T:(b + 1) * T],
                                  d == 0, d == DC - 1)
                last.then_inc(k_ps, 1)
                if b >= 1:
                    pe.wait_ge(v_done, b)
                for kt in range(TB):
                    for d in range(DC):
                        tok = b * T + kt * P
                        last = mm(bank(6 + kt // 2)[:, (kt % 2) * D:(kt % 2 + 1) * D], ctx_sb[:, d, tok:tok + P],
                                  wkv_sb[:, d, D:2 * D], d == 0, d == DC - 1)
                last.then_inc(v_ps, 1)
                pe.wait_ge(rows_done, b + 1)
                if b >= 1:
                    pe.wait_ge(rowsT_sb, b)
                for t in range(TB):
                    for c in range(DC):
                        last = nc.tensor.transpose(bank(c)[:, t * P:(t + 1) * P],
                                                   rows[:, b * TB + t, c * P:(c + 1) * P], ident[:, :])
                last.then_inc(rowsT_ps, 1)
                pe.wait_ge(rowsT_sb, b + 1)
                if b >= 1:
                    pe.wait_ge(resid_done, 2 * b)
                for c in range(DC):
                    for d in range(DC):
                        last = mm(bank(2 + c), wq_sb[:, d, c * P:(c + 1) * P], xnT[:, d, b * T:(b + 1) * T],
                                  d == 0, d == DC - 1)
                last.then_inc(q_ps, 1)

            def max_tile(w, i, s, waits):
                p = i // 2
                if i % 2 == 0 and waits(p):
                    pe.wait_ge(max_done, 8 * w + p - 1)
                h, qt = i // TB, i % TB
                last = mm(bank(2 * (p % 2) + i % 2), q_unit[0:KROWS, s, h, qt * P:(qt + 1) * P],
                          k_unit[0:KROWS, s, h, :])
                if i % 2 == 1:
                    last.then_inc(pair_ps, 1)

            def turn_max(w, s):
                pe.wait_ge(max_done, 8 * w + 8)
                nc.tensor.transpose(bank(7)[:, 0:P], neg_max[:, s, :], ident[:, :]).then_inc(nmT_ps, 1)

            def pv(u, s, kt, first=False):
                pe.wait_ge(exp_done, u * TB * HG + kt * HG + HG)
                if kt == 0 and not first:
                    pe.wait_ge(o_done, u)
                for h in range(HG):
                    last = mm(bank(6)[h * VW:(h + 1) * VW, :], v_unit[:, s, kt, h * VW:(h + 1) * VW],
                              probs[:, (kt * HG + h) % 8, :], kt == 0, kt == TB - 1)
                last.then_inc(pv_done, 1)

            def turn_out(u, s):
                pe.wait_ge(o_done, u + 1)
                for qt in range(TB):
                    last = nc.tensor.transpose(bank(7)[:, qt * P:(qt + 1) * P], o_sb[:, s, qt * P:(qt + 1) * P],
                                               ident[:, :])
                last.then_inc(oT_ps, 1)

            def slot(u, bu, r, first=False, more_max=True, more_turn=True):
                s, w = r % NG, (r + 2) % NG
                if more_max:
                    pe.wait_ge(unit_in[w], 16 * LOADS * (bu + (r + 2) // NG + 1))
                pe.wait_ge(nm_in[s], 16 * MROWS * (bu + r // NG + 1))
                for k in range(TB * HG):
                    kt, h = k // HG, k % HG
                    if not (first and k < 2):
                        pe.wait_ge(exp_done, u * TB * HG + k - 1)
                    mm(bank(4 + k % 2), k_unit[0:KROWS + MROWS, s, h, kt * P:(kt + 1) * P],
                       q_unit[0:KROWS + MROWS, s, h, :]).then_inc(score_ps, 1)
                    if more_max:
                        max_tile(u + 2, k, w, lambda p: True)
                    if k == 3 and not first:
                        pv(u - 1, (r - 1) % NG, TB - 1)
                    if k == 4 and more_turn:
                        if first:
                            pe.wait_ge(nmT_sb, 1)
                        else:
                            pe.wait_ge(attn_rows, u)
                        turn_max(u + 1, (r + 1) % 2)
                    if k >= 7 and k % HG == HG - 1:
                        pv(u, s, kt - 1, first)
                    if k == 9 and not first:
                        if more_turn:
                            pe.wait_ge(nmT_sb, u + 2)
                        else:
                            pe.wait_ge(attn_rows, u)
                        turn_out(u - 1, (r - 1) % 2)

            pe.wait_ge(ones_rows, 1)
            pe.wait_ge(const_step, 3)
            pe.wait_ge(rowsT_sb, B)
            pe.wait_ge(resid_done, 2 * B)
            pe.wait_ge(v_done, B)
            for w in range(2):
                pe.wait_ge(unit_in[w], 16 * LOADS)
                for i in range(16):
                    max_tile(w, i, w, lambda p, w=w: w > 0 or p >= 2)
                if w == 0:
                    turn_max(0, 0)
            slot(0, 0, 0, first=True)
            with pe.Fori(0, B - 1) as b:
                for r in range(1, NG + 1):
                    slot(b * NG + r, b, r)
            for u in range(UNITS - 3, UNITS):
                slot(u, u // NG, u % NG, more_max=u + 2 < UNITS, more_turn=u + 1 < UNITS)
            pv(UNITS - 1, (UNITS - 1) % NG, TB - 1)
            pe.wait_ge(attn_rows, UNITS)
            turn_out(UNITS - 1, (UNITS - 1) % 2)

            pe.wait_ge(small_in, 16 * 5)
            pe.wait_ge(attn_rows, UNITS + 1)
            def proj(t):
                pe.wait_ge(atT_sb, t + 1)
                if t >= 2:
                    pe.wait_ge(x1_done, t - 1)
                for c in range(DC):
                    last = mm(bank(2 + t % 2)[:, 0:D], attnT[:, t % 2, c, :], wp_sb[:, c, :], c == 0, c == DC - 1)
                last.then_inc(proj_ps, 1)

            for t in range(NT):
                if t >= 2:
                    pe.wait_ge(atT_sb, t - 1)
                for c in range(DC):
                    last = nc.tensor.transpose(bank(t % 2)[:, c * P:(c + 1) * P], rows[:, t, c * P:(c + 1) * P],
                                               ident[:, :])
                last.then_inc(atT_ps, 1)
                if t >= 1:
                    proj(t - 1)
            proj(NT - 1)
            for b in range(B):
                pe.wait_ge(rows_done, B + b + 1)
                if b >= 2:
                    pe.wait_ge(rowsT_sb, B + b - 1)
                for t in range(TB):
                    for c in range(DC):
                        last = nc.tensor.transpose(bank(4 + 2 * (b % 2) + c)[:, t * P:(t + 1) * P],
                                                   rows[:, b * TB + t, c * P:(c + 1) * P], ident[:, :])
                last.then_inc(rowsT_ps, 1)
                pe.wait_ge(rowsT_sb, B + b + 1)
                for t in range(b * TB, (b + 1) * TB):
                    for c in range(DC):
                        last = mm(bank(0)[:, t * E:(t + 1) * E], xnT[:, c, t * P:(t + 1) * P], gate_sb[:, c, :],
                                  c == 0, c == DC - 1)
            last.then_inc(logit_ps, 1)
            pe.wait_ge(chosen_done, 3)
            mm(bank(1)[:, 0:1], chosen[:, :, :].rearrange("p t e -> p (t e)"), ones_bf[:, 0:1]).then_inc(totals_ps, 1)
            pe.wait_ge(totals_sb, 1)
            pe.wait_ge(const_step, 8)
            mm(bank(2)[:, 0:NT * E], before[:, :], chosen[:, :, :].rearrange("p t e -> p (t e)"), True, False)
            mm(bank(2)[:, 0:NT * E], totals[:, :], before_tile[:, :, :].rearrange("p t e -> p (t e)"), False, True)
            mm(bank(3)[:, 0:E], totals[:, :], same_e_bf[:, :]).then_inc(rank_ps, 1)

            def shared(i, first):
                for f in range(FC):
                    if not first:
                        pe.wait_ge(sh_hid, FC * i + f - FC + 1)
                    for half in range(2):
                        for c in range(DC):
                            col = half * HALF + f * P
                            last = mm(bank(3 * half + f), w_up[:, E, c, col:col + P], xnT[:, c, bass.ds(i * T, T)],
                                      c == 0, c == DC - 1)
                    last.then_inc(sh_up_ps, 1)
                pe.wait_ge(sh_hid, FC * i + FC)
                for q in range(2):
                    if not first:
                        pe.wait_ge(sh_added, 2 * i + q - 1)
                    for t in range(2):
                        for f in range(FC):
                            tok = (2 * q + t) * P
                            last = mm(bank(6 + q)[:, t * D:(t + 1) * D], sh_hT[:, f, tok:tok + P], w_dn[:, E, f, :],
                                      f == 0, f == FC - 1)
                    last.then_inc(sh_y_ps, 1)

            pe.wait_ge(w_ffn_in, 16 * 2 * (E + 1))
            pe.wait_ge(slots_done, 1)
            shared(0, True)
            with pe.Fori(1, B) as i:
                shared(i, False)

            def expert(j):
                return pe.value_load(block_ei[0:1, bass.ds(j, 1)], min_val=0, max_val=E - 1)

            def turn_x(j, s, half, first=False):
                pe.wait_ge(bx_in[s], 16 * (half + 1))
                if not first:
                    pe.wait_ge(bxT_sb, j)
                for c in range(DC):
                    last = nc.tensor.transpose(bank(4)[:, c * P:(c + 1) * P], blk_x[:, s, c * P:(c + 1) * P],
                                               ident[:, :])
                last.then_inc(bxT_ps, 1)

            def up(j, s, first=False):
                e = expert(j)
                pe.wait_ge(bxT_sb, j + 1)
                if not first:
                    pe.wait_ge(bhid, j - 1)
                for c in range(DC):
                    for g in range(2):
                        last = mm(bank(2 * s + g)[:, 0:HALF], blk_xT[:, s, c, :],
                                  w_up[:, bass.ds(e, 1), c, g * HALF:(g + 1) * HALF].rearrange("p a f -> p (a f)"),
                                  c == 0, c == DC - 1)
                last.then_inc(bup_ps, 1)

            def turn_h(j, first=False):
                pe.wait_ge(bhid, j + 1)
                if not first:
                    pe.wait_ge(bhT_sb, j)
                for f in range(FC):
                    last = nc.tensor.transpose(bank(5)[:, f * P:(f + 1) * P], blk_h[:, f * P:(f + 1) * P], ident[:, :])
                last.then_inc(bhT_ps, 1)

            def down(j, s, first=False):
                e = expert(j)
                pe.wait_ge(bhT_sb, j + 1)
                if not first:
                    pe.wait_ge(by_sb, j - 1)
                for f in range(FC):
                    last = mm(bank(6 + s)[:, 0:D], blk_hT[:, f, :],
                              w_dn[:, bass.ds(e, 1), f, :].rearrange("p a n -> p (a n)"), f == 0, f == FC - 1)
                last.then_inc(by_ps, 1)

            pe.wait_ge(slots_done, 2)
            pe.wait_ge(sh_added, 2 * B)
            turn_x(0, 0, 0, first=True)
            turn_x(1, 1, 0)
            up(0, 0, first=True)
            turn_h(0, first=True)
            turn_x(2, 0, 1)
            up(1, 1, first=True)
            down(0, 0, first=True)
            turn_h(1)
            turn_x(3, 1, 1)
            up(2, 0)
            down(1, 1, first=True)
            with pe.Fori(0, (MAX_BLOCKS - 5) // 2) as i:
                for q in range(2):
                    turn_h(i * 2 + 2 + q)
                    turn_x(i * 2 + 4 + q, q, i + 2)
                    up(i * 2 + 3 + q, (1 + q) % 2)
                    down(i * 2 + 2 + q, q)
            for j in range(2 + 2 * ((MAX_BLOCKS - 5) // 2), MAX_BLOCKS):
                turn_h(j)
                if j + 2 < MAX_BLOCKS:
                    turn_x(j + 2, j % 2, (j + 2) // 2)
                if j + 1 < MAX_BLOCKS:
                    up(j + 1, (j + 1) % 2)
                down(j, j % 2)


def kernel(x, ctx_1024, g_xattn, g_ffn, L0_xattn_W_kv, L0_xattn_W_q, L0_xattn_W_proj, L0_xattn_b_proj,
           L0_ffn_gate_w, L0_ffn_w_up, L0_ffn_w_down, L0_ffn_sg_gate, L0_ffn_sg_up, L0_ffn_sg_down):
    import concourse.bacc as bacc
    from concourse.bass_utils import run_bass_kernel_spmd

    def arr(a):
        return np.asarray(a)

    shared_up = np.concatenate([arr(L0_ffn_sg_gate), arr(L0_ffn_sg_up)], axis=0)[None]
    host = {
        "x": arr(x),
        "ctxT": arr(ctx_1024).reshape(N, D).T,
        "g_xattn": arr(g_xattn),
        "g_ffn": arr(g_ffn),
        "w_kv": arr(L0_xattn_W_kv),
        "w_q": arr(L0_xattn_W_q),
        "w_proj": arr(L0_xattn_W_proj),
        "b_proj": arr(L0_xattn_b_proj),
        "gateT": arr(L0_ffn_gate_w).T,
        "w_upT": np.concatenate([arr(L0_ffn_w_up), shared_up], axis=0).transpose(0, 2, 1),
        "w_downT": np.concatenate([arr(L0_ffn_w_down), arr(L0_ffn_sg_down)[None]], axis=0).transpose(0, 2, 1),
    }
    host = {k: np.ascontiguousarray(v) for k, v in host.items()}
    nc = bacc.Bacc("TRN2", target_bir_lowering=False, num_devices=1)
    args = [nc.dram_tensor(f"in_{k}", v.shape, mybir.dt.from_np(v.dtype), kind="ExternalInput").ap()
            for k, v in host.items()]
    out = nc.dram_tensor("out", (B, T, D), F32, kind="ExternalOutput").ap()
    build(nc, *args, out)
    r = run_bass_kernel_spmd(nc, [{f"in_{k}": v for k, v in host.items()}], core_ids=[0])
    return r.results[0]["out"]
```

```python
from contextlib import ExitStack

import concourse.bass as bass
import numpy as np
from concourse import mybir

P = 128
F32, BF16, I32, U32 = mybir.dt.float32, mybir.dt.bfloat16, mybir.dt.int32, mybir.dt.uint32
ALU = mybir.AluOpType
ACT = mybir.ActivationFunctionType
AX = mybir.AxisListType

B, T, D = 4, 512, 256
N = B * T
NT = N // P
TB = T // P
DC = D // P
H, HD = 16, 16
HG = 4
NG = H // HG
UNITS = B * NG
VW = 32
E, HALF, FFN = 8, 384, 768
FC = HALF // P
TOPK = 2
MAX_BLOCKS = (TOPK * N + E * (P - 1)) // P
EPS = 1e-5
K_RUNS = ((0, 1, 2), (0,), (0, 1))
Q_RUNS = ((0, 1), (0, 1, 2), (0,))
OUTS = 2 * (H // 4) + 1
K_PARTS, Q_PARTS = sum(K_RUNS, ()), sum(Q_RUNS, ())
assert sorted(zip(K_PARTS, Q_PARTS)) == [(i, j) for i in range(3) for j in range(3 - i)]
KROWS = len(K_PARTS) * HD
MROWS = 3
LOADS = len(K_RUNS) + len(Q_RUNS) + 1


def build(nc, x, ctxT, g_xattn, g_ffn, w_kv, w_q, w_proj, b_proj, gateT, w_upT, w_downT, out):
    qk_parts = nc.dram_tensor("qk_parts", (2, B, NG, 3, HD * HG, T), BF16, kind="Internal").ap()
    v_rows = nc.dram_tensor("v_rows", (B, P, TB, H * VW), F32, kind="Internal").ap()
    x_slots = nc.dram_tensor("x_slots", (MAX_BLOCKS * P, D), F32, kind="Internal").ap()
    y_slots = nc.dram_tensor("y_slots", (MAX_BLOCKS * P, D), F32, kind="Internal").ap()

    x_dram = x.rearrange("b (t p) d -> p (b t) d", p=P)
    out_dram = out.rearrange("b (t p) d -> p (b t) d", p=P)

    with ExitStack() as ctx:
        def sb(name, shape, dt=F32):
            return ctx.enter_context(nc.sbuf_tensor(name, shape, dt))

        def sem(name):
            return ctx.enter_context(nc.semaphore(name))

        x_sb = sb("x_sb", [P, NT, D])
        rows = sb("rows", [P, NT, D])
        xnT = sb("xnT", [P, DC, N])
        ctx_region = sb("ctx_region", [P, DC * N])
        ctx_sb = ctx_region[:, :].rearrange("p (c n) -> p c n", c=DC)
        probs = ctx_region[:, :].rearrange("p (s n) -> p s n", n=T)
        up_region = sb("up_region", [P, (E + 1) * DC * FFN])
        w_up = up_region[:, :].rearrange("p (e c f) -> p e c f", e=E + 1, c=DC)
        dn_region = sb("dn_region", [P, (E + 1) * FC * D])
        w_dn = dn_region[:, :].rearrange("p (e f n) -> p e f n", e=E + 1, f=FC)
        part_words = B * 2 * 3 * DC * T // 2
        parts = up_region[:, 0:part_words].bitcast(BF16).rearrange("p (b a j c n) -> p b a j c n", b=B, a=2, j=3, c=DC)
        resid = dn_region[:, 0:2 * DC * T].rearrange("p (a c n) -> p a c n", a=2, c=DC)
        v_sb = dn_region[:, 2 * DC * T:2 * DC * T + 2 * TB * H * VW].rearrange(
            "p (s k h w) -> p s k h w", s=2, k=TB, h=H)

        unit_words = 2 * 4 * HG * T // 2 + 4 * TB * HG * VW
        unit_region = sb("unit_region", [P, unit_words])
        k_unit = unit_region[:, 0:4 * HG * T // 2].bitcast(BF16).rearrange("p (s h n) -> p s h n", s=4, h=HG)
        q_unit = unit_region[:, 4 * HG * T // 2:4 * HG * T].bitcast(BF16).rearrange(
            "p (s h n) -> p s h n", s=4, h=HG)
        v_unit = unit_region[:, 4 * HG * T:unit_words].rearrange("p (s k c) -> p s k c", s=4, k=TB)
        used = [0]

        def work(words, pattern, **sizes):
            a = used[0]
            used[0] += words
            assert used[0] <= unit_words
            return unit_region[:, a:a + words].rearrange(pattern, **sizes)

        sh_gate = work(FC * T, "p (f n) -> p f n", f=FC)
        sh_hT = work(FC * T, "p (f n) -> p f n", f=FC)
        blk_x = work(2 * D, "p (s d) -> p s d", s=2)
        blk_xT = work(2 * D, "p (s c n) -> p s c n", s=2, c=DC)
        blk_gate = work(HALF, "p f -> p f")
        blk_h = work(HALF, "p f -> p f")
        blk_hT = work(HALF, "p (f n) -> p f n", f=FC)
        blk_y = work(2 * D, "p (s d) -> p s d", s=2)
        attnT = work(2 * D, "p (s c n) -> p s c n", s=2, c=DC)
        logits = work(NT * E, "p (t e) -> p t e", t=NT)
        top8 = work(NT * 8, "p (t e) -> p t e", t=NT)
        onehot = work(2 * NT * E, "p (k t e) -> p k t e", k=2, t=NT)
        rank = work(NT * E, "p (t e) -> p t e", t=NT)
        past = work(MAX_BLOCKS * E, "p (j e) -> p j e", e=E)
        GB = 3
        got = work(GB * 2 * D, "p (s k d) -> p s k d", s=GB, k=2)

        wq_sb = sb("wq_sb", [P, DC, D])
        wkv_sb = sb("wkv_sb", [P, DC, 2 * D])
        wp_sb = sb("wp_sb", [P, DC, D])
        gate_sb = sb("gate_sb", [P, DC, E])
        bias_sb = sb("bias_sb", [P, D])
        gates = sb("gates", [P, 2])
        tanh_g = sb("tanh_g", [P, 2])
        eps_sb = sb("eps_sb", [P, 1])
        ident = sb("ident", [P, P])
        stats = sb("stats", [P, NT, 6])
        mean_var = sb("mean_var", [P, NT, 2])
        std = sb("std", [P, NT])
        rstd = sb("rstd", [P, NT])
        neg_max = sb("neg_max", [P, 2, P])
        nmT = sb("nmT", [HG * TB, P])
        nm_res = sb("nm_res", [HG * TB, P])
        nm_parts = sb("nm_parts", [HG * TB, 3, P], BF16)
        o_sb = sb("o_sb", [P, 2, T])
        rinv = sb("rinv", [P, TB, HG])
        zeros = sb("zeros", [P, D])
        ones_bf = sb("ones_bf", [P, P], BF16)
        before = sb("before", [P, P], BF16)
        before_tile = sb("before_tile", [P, NT, E], BF16)
        same_e = sb("same_e", [P, E])
        same_e_bf = sb("same_e_bf", [P, E], BF16)
        iota_e = sb("iota_e", [P, E])
        iota_b = sb("iota_b", [P, MAX_BLOCKS])
        top8_idx = sb("top8_idx", [P, NT, 8], U32)
        topi = sb("topi", [P, 2, NT])
        chosen = sb("chosen", [P, NT, E], BF16)
        totals = sb("totals", [P, P], BF16)
        count = sb("count", [P, E])
        count_i = sb("count_i", [P, E], I32)
        blocks_i = sb("blocks_i", [P, E], I32)
        blocks = sb("blocks", [P, E])
        ends = sb("ends", [P, E])
        base = sb("base", [P, E])
        block_e = sb("block_e", [P, MAX_BLOCKS])
        block_ei = sb("block_ei", [P, MAX_BLOCKS], I32)
        slot_f = sb("slot_f", [P, 2, NT])
        slot_i = sb("slot_i", [P, 2, NT], I32)
        pexp = sb("pexp", [P, 2, NT])
        wsel = sb("wsel", [P, 2, NT])

        ps = [ctx.enter_context(nc.psum_tensor(f"ps{i}", [P, 4, 512], F32)) for i in range(2)]

        def bank(i, n=1):
            return ps[i // 4][:, i % 4, :] if n == 1 else ps[i // 4][:, i % 4:i % 4 + n, :]

        x_in = [sem(f"x_in{b}") for b in range(B)]
        ctx_in = [sem(f"ctx_in{b}") for b in range(B)]
        w_attn_in, wq_in = sem("w_attn_in"), sem("wq_in")
        small_in = sem("small_in")
        const_step = sem("const_step")
        ident_done = sem("ident_done")
        tanh_done = sem("tanh_done")
        bias_done = sem("bias_done")
        ones_rows = sem("ones_rows")
        v_ones = sem("v_ones")
        resid_base = sem("resid_base")
        stat_done = sem("stat_done")
        var_done = sem("var_done")
        std_done = sem("std_done")
        rstd_done = sem("rstd_done")
        rows_done = sem("rows_done")
        rowsT_ps = sem("rowsT_ps")
        rowsT_sb = sem("rowsT_sb")
        k_ps, v_ps, q_ps = sem("k_ps"), sem("v_ps"), sem("q_ps")
        high_done = sem("high_done")
        resid_done = sem("resid_done")
        v_done = sem("v_done")
        mid_done = sem("mid_done")
        low_done = sem("low_done")
        qkv_out = [sem(f"qkv_out{s}") for s in range(2)]
        unit_in = [sem(f"unit_in{s}") for s in range(4)]
        pair_ps = sem("pair_ps")
        max_done = sem("max_done")
        nmT_ps, nmT_sb = sem("nmT_ps"), sem("nmT_sb")
        nm_step = sem("nm_step")
        nm_split = sem("nm_split")
        nm_in = [sem(f"nm_in{s}") for s in range(4)]
        score_ps = sem("score_ps")
        exp_done = sem("exp_done")
        pv_done = sem("pv_done")
        o_done = sem("o_done")
        oT_ps = sem("oT_ps")
        rinv_done = sem("rinv_done")
        attn_rows = sem("attn_rows")
        w_ffn_in = sem("w_ffn_in")
        zero_out = sem("zero_out")
        atT_ps, atT_sb = sem("atT_ps"), sem("atT_sb")
        proj_ps = sem("proj_ps")
        x1_done = sem("x1_done")
        logit_ps = sem("logit_ps")
        route = sem("route")
        chosen_done = sem("chosen_done")
        totals_ps, totals_sb = sem("totals_ps"), sem("totals_sb")
        rank_ps = sem("rank_ps")
        pexp_done = sem("pexp_done")
        slots_done = sem("slots_done")
        wsel_done = sem("wsel_done")
        scattered = sem("scattered")
        sh_up_ps = sem("sh_up_ps")
        sh_silu = sem("sh_silu")
        sh_hid = sem("sh_hid")
        sh_y_ps = sem("sh_y_ps")
        sh_added = sem("sh_added")
        bx_in = [sem(f"bx_in{s}") for s in range(2)]
        bxT_ps, bxT_sb = sem("bxT_ps"), sem("bxT_sb")
        bup_ps = sem("bup_ps")
        bsilu = sem("bsilu")
        bhid = sem("bhid")
        bhT_ps, bhT_sb = sem("bhT_ps"), sem("bhT_sb")
        by_ps, by_sb = sem("by_ps"), sem("by_sb")
        by_out = [sem(f"by_out{s}") for s in range(2)]
        got_in = [sem(f"got_in{s}") for s in range(GB)]
        added = sem("added")
        out_done = sem("out_done")

        block = ctx.enter_context(nc.Block())

        @block.sync
        def _(sp):
            for b in range(B):
                if b == 0:
                    sp.dma_start(wkv_sb[:, :, :], w_kv.rearrange("(c p) n -> p c n", p=P)).then_inc(w_attn_in, 16)
                sp.dma_start(ctx_sb[:, :, b * T:(b + 1) * T],
                             ctxT.rearrange("(c p) n -> p c n", p=P)[:, :, b * T:(b + 1) * T]).then_inc(ctx_in[b], 16)
                sp.dma_start(x_sb[:, b * TB:(b + 1) * TB, :], x_dram[:, b * TB:(b + 1) * TB, :]).then_inc(x_in[b], 16)
                if b == 0:
                    sp.dma_start(wq_sb[:, :, :], w_q.rearrange("(c p) n -> p c n", p=P)).then_inc(wq_in, 16)
            def load_unit(b, g):
                for a, dst, runs in ((1, k_unit, K_RUNS), (0, q_unit, Q_RUNS)):
                    row = 0
                    for run in runs:
                        n = len(run)
                        src = qk_parts[a, bass.ds(b, 1), g, 0:n, :, :].rearrange("a j (d h) n -> (a j d) (h n)", h=HG)
                        to = dst[row:row + n * HD, g, :, :].rearrange("p h n -> p (h n)")
                        sp.dma_start(to, src).then_inc(unit_in[g], 16)
                        row += n * HD
                src = v_rows[bass.ds(b, 1), :, :, g * HG * VW:(g + 1) * HG * VW].rearrange("a p k c -> p (a k) c")
                sp.dma_start(v_unit[:, g, :, :], src).then_inc(unit_in[g], 16)

            for b in range(B):
                s = b % 2
                for i, a in enumerate((1, 0)):
                    sp.wait_ge(low_done, 2 * b + i + 1)
                    for g in range(NG):
                        half = P // 2 * (g % 2)
                        sp.dma_start(qk_parts[a, b, g, :, :, :].rearrange("j r n -> r j n"),
                                     parts[half:half + P // 2, b, a, :, g // 2, :]).then_inc(qkv_out[s], 16)
                sp.wait_ge(v_done, b + 1)
                sp.dma_start(v_rows[b, :, :, :], v_sb[:, s, :, :, :].rearrange("p k h w -> p k (h w)")
                             ).then_inc(qkv_out[s], 16)
                if b == 1:
                    sp.wait_ge(qkv_out[0], 16 * OUTS)
                    for g in range(NG):
                        load_unit(0, g)
            for s in range(2):
                sp.wait_ge(qkv_out[s], 16 * OUTS * (B // 2))

            def send_max(u, g):
                sp.wait_ge(nm_split, u + 1)
                for j in range(MROWS):
                    dst = q_unit[KROWS + j:KROWS + j + 1, g, :, :].rearrange("a h (t n) -> a (h t) n", n=P)
                    sp.dma_start(dst, nm_parts[:, j, :]).then_inc(nm_in[g], 16)

            send_max(0, 0)
            with sp.Fori(0, B - 1) as b:
                for g in range(NG):
                    send_max(b * NG + g + 1, (g + 1) % NG)
                    sp.wait_ge(pv_done, (b * NG + g) * TB + TB)
                    load_unit(b + 1, g)
            for u in range(UNITS - 3, UNITS):
                send_max(u, u % NG)

            def load_block(j, s):
                sp.dma_start(blk_x[:, s, :], x_slots[bass.ds(j * P, P), :]).then_inc(bx_in[s], 16)

            def store_block(j, s):
                sp.wait_ge(by_sb, j + 1)
                sp.dma_start(y_slots[bass.ds(j * P, P), :], blk_y[:, s, :]).then_inc(by_out[s], 16)

            sp.wait_ge(zero_out, 16)
            sp.wait_ge(scattered, 16 * 2 * NT)
            load_block(0, 0)
            load_block(1, 1)
            for j in (2, 3):
                sp.wait_ge(bxT_ps, j - 1)
                load_block(j, j % 2)

            def sp_block(j, s, load):
                if load:
                    sp.wait_ge(bxT_ps, j + 3)
                    load_block(j + 4, s)
                store_block(j, s)

            sp_block(0, 0, True)
            PAIRS = (MAX_BLOCKS - 5) // 2
            with sp.Fori(0, PAIRS) as i:
                sp_block(i * 2 + 1, 1, True)
                sp_block(i * 2 + 2, 0, True)
            for j in range(1 + 2 * PAIRS, MAX_BLOCKS):
                sp_block(j, j % 2, j + 4 < MAX_BLOCKS)
            for t in range(NT):
                sp.wait_ge(added, t + 1)
                sp.dma_start(out_dram[:, t, :], x_sb[:, t, :]).then_inc(out_done, 16)
            sp.wait_ge(out_done, 16 * NT)

        @block.gpsimd
        def _(pool):
            nc.gpsimd.memset(ident[:, :], 0.0).then_inc(const_step, 1)
            pool.wait_ge(const_step, 1)
            nc.gpsimd.affine_select(out=ident[:, :], in_=ident[:, :], compare_op=ALU.not_equal, fill=1.0, base=0,
                                    pattern=[[-1, P]], channel_multiplier=1).then_inc(ident_done, 1)
            pool.wait_ge(ident_done, 1)
            nc.gpsimd.memset(zeros[:, :], 0.0).then_inc(const_step, 1)
            pool.wait_ge(const_step, 2)
            nc.gpsimd.memset(neg_max[:, :, :], 0.0).then_inc(const_step, 1)
            pool.wait_ge(const_step, 3)
            nc.gpsimd.memset(ones_bf[:, :], 1.0).then_inc(const_step, 1)
            pool.wait_ge(const_step, 4)
            nc.gpsimd.affine_select(out=before[:, :], in_=ones_bf[:, :], compare_op=ALU.is_gt, fill=0.0, base=0,
                                    pattern=[[1, P]], channel_multiplier=-1).then_inc(const_step, 1)
            pool.wait_ge(const_step, 5)
            nc.gpsimd.iota(iota_e[:, :], pattern=[[1, E]], base=0, channel_multiplier=0,
                           allow_small_or_imprecise_dtypes=True).then_inc(const_step, 1)
            pool.wait_ge(const_step, 6)
            nc.gpsimd.iota(iota_b[:, :], pattern=[[1, MAX_BLOCKS]], base=0, channel_multiplier=0,
                           allow_small_or_imprecise_dtypes=True).then_inc(const_step, 1)
            pool.wait_ge(const_step, 7)
            nc.gpsimd.memset(v_sb[:, :, :, :, HD:VW], 1.0).then_inc(v_ones, 1)
            pool.wait_ge(v_ones, 1)
            nc.gpsimd.memset(k_unit[KROWS:KROWS + MROWS, :, :, :], 1.0).then_inc(ones_rows, 1)
            pool.wait_ge(ones_rows, 1)
            pool.wait_ge(route, 2)
            nc.gpsimd.affine_select(out=before_tile[:, :, :], in_=before_tile[:, :, :], compare_op=ALU.is_gt,
                                    fill=0.0, base=0, pattern=[[E, NT], [1, E]], channel_multiplier=-1
                                    ).then_inc(const_step, 1)
            pool.wait_ge(const_step, 8)
            pool.wait_ge(bias_done, 1)
            for t in range(NT):
                pool.wait_ge(rows_done, t // TB + 1)
                nc.gpsimd.tensor_tensor(x_sb[:, t, :], x_sb[:, t, :], bias_sb[:, :], ALU.add).then_inc(resid_base, 1)
            pool.wait_ge(resid_base, NT)

            def split_max(u):
                pool.wait_ge(nmT_sb, u + 1)
                if u >= 1:
                    pool.wait_ge(nm_in[(u - 1) % NG], 16 * MROWS * ((u - 1) // NG + 1))
                nc.gpsimd.tensor_copy(nm_parts[:, 0, :], nmT[:, :]).then_inc(nm_step, 1)
                pool.wait_ge(nm_step, 3 * u + 1)
                nc.gpsimd.tensor_tensor(nm_res[:, :], nmT[:, :], nm_parts[:, 0, :], ALU.subtract).then_inc(nm_step, 1)
                pool.wait_ge(nm_step, 3 * u + 2)
                nc.gpsimd.tensor_copy(nm_parts[:, 1, :], nm_res[:, :]).then_inc(nm_step, 1)
                pool.wait_ge(nm_step, 3 * u + 3)
                nc.gpsimd.tensor_tensor(nm_parts[:, 2, :], nm_res[:, :], nm_parts[:, 1, :], ALU.subtract
                                        ).then_inc(nm_split, 1)
                pool.wait_ge(nm_split, u + 1)

            for u in range(UNITS):
                split_max(u)

            pool.wait_ge(slots_done, 1)
            pool.wait_ge(zero_out, 16)
            for t in range(NT):
                for k in range(TOPK):
                    pool.indirect_dma_start(
                        out=x_slots[:, :], out_offset=bass.IndirectOffsetOnAxis(ap=slot_i[:, k, t:t + 1], axis=0),
                        in_=rows[:, t, :], in_offset=None).then_inc(scattered, 16)
            for s in range(2):
                pool.wait_ge(by_out[s], 16 * ((MAX_BLOCKS + 1 - s) // 2))
            for t in range(NT):
                if t >= GB:
                    pool.wait_ge(added, t - GB + 1)
                for k in range(TOPK):
                    pool.indirect_dma_start(
                        out=got[:, t % GB, k, :], out_offset=None, in_=y_slots[:, :],
                        in_offset=bass.IndirectOffsetOnAxis(ap=slot_i[:, k, t:t + 1], axis=0)
                        ).then_inc(got_in[t % GB], 16)

        @block.scalar
        def _(act):
            act.dma_start(gates[:, 0:1], g_xattn.partition_broadcast(P)).then_inc(small_in, 16)
            act.dma_start(gates[:, 1:2], g_ffn.partition_broadcast(P)).then_inc(small_in, 16)
            act.dma_start(bias_sb[:, :], b_proj.partition_broadcast(P)).then_inc(small_in, 16)
            act.dma_start(wp_sb[:, :, :], w_proj.rearrange("(c p) n -> p c n", p=P)).then_inc(small_in, 16)
            act.dma_start(gate_sb[:, :, :], gateT.rearrange("(c p) n -> p c n", p=P)).then_inc(small_in, 16)
            act.wait_ge(small_in, 16 * 5)
            nc.scalar.activation(tanh_g[:, :], gates[:, :], ACT.Tanh).then_inc(tanh_done, 1)

            def std_of(b, n):
                act.wait_ge(var_done, n)
                nc.scalar.activation(std[:, b * TB:(b + 1) * TB], mean_var[:, b * TB:(b + 1) * TB, 1], ACT.Sqrt,
                                     bias=eps_sb[:, 0:1]).then_inc(std_done, 1)

            def mid_part(b, a):
                act.wait_ge(resid_done, 2 * b + 2 - a)
                nc.scalar.copy(parts[:, b, a, 1, :, :], resid[:, a, :, :]).then_inc(mid_done, 1)

            for b in range(B):
                std_of(b, b + 1)
            for b in range(B):
                s = b % 2
                act.wait_ge(rowsT_ps, b + 1)
                nc.scalar.copy(xnT[:, :, b * T:(b + 1) * T], bank(0, 2)).then_inc(rowsT_sb, 1)
                act.wait_ge(k_ps, b + 1)
                nc.scalar.copy(parts[:, b, 1, 0, :, :], bank(4, 2)).then_inc(high_done, 1)
                if b >= 1:
                    mid_part(b - 1, 0)
                act.wait_ge(v_ps, b + 1)
                if b == 0:
                    act.wait_ge(v_ones, 1)
                if b >= 2:
                    act.wait_ge(qkv_out[s], 16 * OUTS * (b // 2))
                nc.scalar.copy(v_sb[:, s, :, :, 0:HD],
                               bank(6, 2).rearrange("p a (k h w) -> p (a k) h w", k=2, h=H)).then_inc(v_done, 1)
                mid_part(b, 1)
                act.wait_ge(q_ps, b + 1)
                nc.scalar.mul(parts[:, b, 0, 0, :, :], bank(2, 2), float(HD) ** -0.5).then_inc(high_done, 1)
            mid_part(B - 1, 0)
            for s in range(2):
                act.wait_ge(qkv_out[s], 16 * OUTS * (B // 2))
            act.wait_ge(const_step, 2)

            def load_expert(e):
                act.dma_start(w_up[:, bass.ds(e, 1), :, :].rearrange("p a c f -> p (a c) f"),
                              w_upT[bass.ds(e, 1), :, :].rearrange("a (c p) f -> p (a c) f", p=P)).then_inc(w_ffn_in, 16)
                act.dma_start(w_dn[:, bass.ds(e, 1), :, :].rearrange("p a c n -> p (a c) n"),
                              w_downT[bass.ds(e, 1), :, :].rearrange("a (c p) n -> p (a c) n", p=P)
                              ).then_inc(w_ffn_in, 16)

            def copy_max(u):
                if not isinstance(u, int) or u >= 1:
                    act.wait_ge(nm_split, u)
                act.wait_ge(nmT_ps, u + 1)
                nc.scalar.copy(nmT[:, :], bank(7)[0:HG * TB, 0:P]).then_inc(nmT_sb, 1)

            def copy_out(u, s):
                act.wait_ge(pv_done, u * TB + TB)
                nc.scalar.copy(o_sb[:, s, :], bank(6)).then_inc(o_done, 1)

            def exp_slot(u, g, first=False, more_max=True):
                for k in range(TB * HG):
                    kt = k // HG
                    if k % HG == 0 and not (first and kt < 2):
                        act.wait_ge(pv_done, u * TB + kt - 1)
                    act.wait_ge(score_ps, u * TB * HG + k + 1)
                    nc.scalar.activation(probs[:, k % 8, :], bank(4 + k % 2), ACT.Exp).then_inc(exp_done, 1)
                    if k == 3 and not first:
                        copy_out(u - 1, (g + 1) % 2)
                    if k == 4 and more_max:
                        copy_max(u + 1)

            copy_max(0)
            exp_slot(0, 0, first=True)
            with act.Fori(0, B - 1) as b:
                for r in range(1, NG + 1):
                    if r < NG:
                        load_expert(b * 3 + r - 1)
                    exp_slot(b * NG + r, r % NG)
            act.dma_start(x_slots.rearrange("(j p) d -> p j d", p=P),
                          zeros[:, :].unsqueeze(1).to_broadcast([P, MAX_BLOCKS, D])).then_inc(zero_out, 16)
            for u in range(UNITS - 3, UNITS):
                exp_slot(u, u % NG, more_max=u + 1 < UNITS)
            copy_out(UNITS - 1, (UNITS - 1) % 2)

            def copy_attnT(b):
                for t in range(b * TB, (b + 1) * TB):
                    act.wait_ge(atT_ps, t + 1)
                    if t >= 2:
                        act.wait_ge(proj_ps, t - 1)
                    nc.scalar.copy(attnT[:, t % 2, :, :], bank(t % 2)[:, 0:D].rearrange("p (c n) -> p c n", c=DC)
                                   ).then_inc(atT_sb, 1)

            def copy_rowsT(b):
                act.wait_ge(rowsT_ps, B + b + 1)
                nc.scalar.copy(xnT[:, 0, b * T:(b + 1) * T], bank(2))
                nc.scalar.copy(xnT[:, 1, b * T:(b + 1) * T], bank(5)).then_inc(rowsT_sb, 1)

            copy_attnT(0)
            copy_attnT(1)
            std_of(0, B + 1)
            copy_rowsT(0)
            copy_attnT(2)
            std_of(1, B + 2)
            copy_rowsT(1)
            copy_attnT(3)
            std_of(2, B + 3)
            copy_rowsT(2)
            std_of(3, B + 4)
            copy_rowsT(3)
            act.wait_ge(route, 3)
            nc.scalar.activation(pexp[:, 1, :], pexp[:, 0, :], ACT.Exp).then_inc(pexp_done, 1)

            def shared_silu(i, f):
                act.wait_ge(sh_up_ps, FC * i + f + 1)
                if not isinstance(i, int) or i >= 1:
                    act.wait_ge(sh_hid, FC * i + f - FC + 1)
                nc.scalar.activation(sh_gate[:, f, :], bank(f), ACT.Silu).then_inc(sh_silu, 1)

            for f in range(FC):
                shared_silu(0, f)
            with act.Fori(1, B) as i:
                for f in range(FC):
                    shared_silu(i, f)

            def block_silu(j, first=False):
                act.wait_ge(bup_ps, 2 * j + 1)
                if not first:
                    act.wait_ge(bhid, j)
                nc.scalar.activation(blk_gate[:, :], blk_gu_bank(j, 0), ACT.Silu).then_inc(bsilu, 1)

            def blk_gu_bank(j, which):
                return bank(2 * par[0] + which)[:, 0:HALF]

            def block_hT(j, first=False):
                act.wait_ge(bhT_ps, j + 1)
                if not first:
                    act.wait_ge(by_ps, j)
                nc.scalar.copy(blk_hT[:, :, :], bank(5)[:, 0:HALF].rearrange("p (f n) -> p f n", f=FC)
                               ).then_inc(bhT_sb, 1)

            par = [0]
            block_silu(0, first=True)
            block_hT(0, first=True)
            par[0] = 1
            block_silu(1)
            with act.Fori(0, (MAX_BLOCKS - 3) // 2) as i:
                for q in range(2):
                    block_hT(i * 2 + 1 + q)
                    par[0] = q
                    block_silu(i * 2 + 2 + q)
            block_hT(MAX_BLOCKS - 2)
            par[0] = (MAX_BLOCKS - 1) % 2
            block_silu(MAX_BLOCKS - 1)
            block_hT(MAX_BLOCKS - 1)

        @block.vector
        def _(dve):
            nc.vector.memset(eps_sb[:, :], EPS)
            dve.sem_inc(attn_rows, 1)

            def ln_stats(b, n):
                for t in range(b * TB, (b + 1) * TB):
                    last = nc.vector.bn_stats(stats[:, t, :], x_sb[:, t, :])
                last.then_inc(stat_done, 1)
                dve.wait_ge(stat_done, n)
                for t in range(b * TB, (b + 1) * TB):
                    last = nc.vector.bn_aggr(mean_var[:, t, :], stats[:, t, :])
                last.then_inc(var_done, 1)

            def ln_apply(b, n):
                dve.wait_ge(std_done, n)
                nc.vector.reciprocal(rstd[:, b * TB:(b + 1) * TB], std[:, b * TB:(b + 1) * TB]).then_inc(rstd_done, 1)
                dve.wait_ge(rstd_done, n)
                for t in range(b * TB, (b + 1) * TB):
                    last = nc.vector.tensor_scalar(rows[:, t, :], x_sb[:, t, :], mean_var[:, t, 0:1],
                                                   rstd[:, t:t + 1], ALU.subtract, ALU.mult)
                last.then_inc(rows_done, 1)

            for b in range(B):
                dve.wait_ge(x_in[b], 16)
                ln_stats(b, b + 1)
            for b in range(B):
                ln_apply(b, b + 1)
            dve.wait_ge(tanh_done, 1)
            nc.vector.tensor_scalar(bias_sb[:, :], bias_sb[:, :], tanh_g[:, 0:1], None, ALU.mult
                                    ).then_inc(bias_done, 1)

            def low_part(i):
                b, a = i // 2, 1 - i % 2
                dve.wait_ge(mid_done, i + 1)
                nc.vector.tensor_tensor(parts[:, b, a, 2, :, :], resid[:, a, :, :], parts[:, b, a, 1, :, :],
                                        ALU.subtract).then_inc(low_done, 1)

            n = 0
            for b in range(B):
                for a, first_bank, scale in ((1, 4, 1.0), (0, 2, float(HD) ** -0.5)):
                    n += 1
                    dve.wait_ge(high_done, n)
                    if n >= 3:
                        dve.wait_ge(low_done, n - 2)
                    for c in range(DC):
                        last = nc.vector.scalar_tensor_tensor(resid[:, a, c, :], bank(first_bank + c), scale,
                                                              parts[:, b, a, 0, c, :], ALU.mult, ALU.subtract)
                    last.then_inc(resid_done, 1)
                    if n >= 2:
                        low_part(n - 2)
                if b == 0:
                    dve.wait_ge(ident_done, 1)
                    nc.vector.tensor_reduce(same_e[:, :], ident[:, :].rearrange("p (t e) -> p e t", e=E), AX.X,
                                            ALU.add).then_inc(route, 1)
                    dve.wait_ge(route, 1)
                    nc.vector.tensor_copy(same_e_bf[:, :], same_e[:, :])
                    nc.vector.tensor_copy(before_tile[:, :, :],
                                          same_e[:, :].unsqueeze(1).to_broadcast([P, NT, E])).then_inc(route, 1)

            low_part(2 * B - 1)

            def max_pair(w, p, s):
                dve.wait_ge(pair_ps, 8 * w + p + 1)
                nc.vector.tensor_reduce(neg_max[:, s, 2 * p:2 * p + 2], bank(2 * (p % 2), 2), AX.X, ALU.max,
                                        negate=True).then_inc(max_done, 1)

            def normalise(u, b, g):
                dve.wait_ge(oT_ps, u + 1)
                o4 = bank(7).rearrange("p (t h w) -> p t h w", t=TB, h=HG)
                nc.vector.reciprocal(rinv[:, :, :], o4[:, :, :, HD]).then_inc(rinv_done, 1)
                dve.wait_ge(rinv_done, u + 1)
                dst = rows[:, bass.ds(b * TB, TB), g * HG * HD:(g + 1) * HG * HD].rearrange(
                    "p t (h w) -> p t h w", h=HG)
                nc.vector.tensor_tensor(dst, o4[:, :, :, 0:HD],
                                        rinv[:, :, :].unsqueeze(3).to_broadcast([P, TB, HG, HD]), ALU.mult
                                        ).then_inc(attn_rows, 1)

            dve.wait_ge(const_step, 3)
            for w in range(2):
                for p in range(8):
                    max_pair(w, p, w)
            for p in range(8):
                max_pair(2, p, 0)

            def dve_slot(u, bu, gu, s, more_max):
                for p in range(8):
                    if more_max:
                        max_pair(u + 2, p, s)
                    if p == 6:
                        normalise(u - 1, bu, gu)

            with dve.Fori(0, B - 1) as b:
                for r in range(1, NG + 1):
                    dve_slot(b * NG + r, b, r - 1, r % 2, True)
            for u in range(UNITS - 3, UNITS + 1):
                dve_slot(u, (u - 1) // NG, (u - 1) % NG, u % 2, u + 2 < UNITS)

            def residual(b):
                for t in range(b * TB, (b + 1) * TB):
                    dve.wait_ge(proj_ps, t + 1)
                    nc.vector.scalar_tensor_tensor(x_sb[:, t, :], bank(3 + t % 2)[:, 0:D], tanh_g[:, 0:1],
                                                   x_sb[:, t, :], ALU.mult, ALU.add).then_inc(x1_done, 1)

            def stats2(b):
                dve.wait_ge(x1_done, (b + 1) * TB)
                ln_stats(b, B + b + 1)

            dve.wait_ge(resid_base, NT)
            residual(0)
            stats2(0)
            residual(1)
            ln_apply(0, B + 1)
            stats2(1)
            residual(2)
            ln_apply(1, B + 2)
            stats2(2)
            residual(3)
            ln_apply(2, B + 3)
            stats2(3)
            ln_apply(3, B + 4)

            def shared_hidden(i, first):
                for f in range(FC):
                    dve.wait_ge(sh_silu, FC * i + f + 1)
                    if not first:
                        dve.wait_ge(sh_y_ps, 2 * i)
                    nc.vector.tensor_tensor(sh_hT[:, f, :], sh_gate[:, f, :], bank(3 + f), ALU.mult
                                            ).then_inc(sh_hid, 1)

            def shared_added(i):
                for q in range(2):
                    dve.wait_ge(sh_y_ps, 2 * i + q + 1)
                    dst = x_sb[:, bass.ds(i * TB + 2 * q, 2), :]
                    nc.vector.scalar_tensor_tensor(dst, bank(6 * q).rearrange("p (t d) -> p t d", t=2),
                                                   tanh_g[:, 1:2], dst, ALU.mult, ALU.add).then_inc(sh_added, 1)

            r = [2]

            def step(ins):
                r[0] += 1
                ins.then_inc(route, 1)
                dve.wait_ge(route, r[0])

            dve.wait_ge(logit_ps, B)
            nc.vector.tensor_copy(logits[:, :, :], bank(7)[:, 0:NT * E].rearrange("p (t e) -> p t e", e=E)
                                  ).then_inc(chosen_done, 1)
            dve.wait_ge(chosen_done, 1)
            for t in range(NT):
                last = nc.vector.max(top8[:, t, :], logits[:, t, :])
            last.then_inc(chosen_done, 1)
            dve.wait_ge(chosen_done, 2)
            step(nc.vector.tensor_tensor(pexp[:, 0, :], top8[:, :, 1], top8[:, :, 0], ALU.subtract))
            for t in range(NT):
                last = nc.vector.max_index(top8_idx[:, t, :], top8[:, t, :], logits[:, t, :])
            step(last)
            step(nc.vector.tensor_copy(topi[:, :, :], top8_idx[:, :, 0:2].rearrange("p t k -> p k t")))
            for k in range(TOPK):
                last = nc.vector.tensor_tensor(onehot[:, k, :, :], topi[:, k, :].unsqueeze(2).to_broadcast([P, NT, E]),
                                               iota_e[:, :].unsqueeze(1).to_broadcast([P, NT, E]), ALU.is_equal)
            step(last)
            nc.vector.tensor_tensor(chosen[:, :, :], onehot[:, 0, :, :], onehot[:, 1, :, :], ALU.add
                                    ).then_inc(chosen_done, 1)
            dve.wait_ge(totals_ps, 1)
            nc.vector.tensor_copy(totals[:, :], bank(7)[:, 128:129].to_broadcast([P, P])).then_inc(totals_sb, 1)
            shared_hidden(0, True)
            dve.wait_ge(rank_ps, 1)
            nc.vector.tensor_copy(rank[:, :, :], bank(7)[:, 256:256 + NT * E].rearrange("p (t e) -> p t e", e=E))
            step(nc.vector.tensor_copy(count[:, :], bank(7)[:, 384:384 + E]))
            step(nc.vector.tensor_scalar(count_i[:, :], count[:, :], float(P - 1), None, ALU.add))
            step(nc.vector.tensor_scalar(blocks_i[:, :], count_i[:, :], 7, None, ALU.logical_shift_right))
            step(nc.vector.tensor_copy(blocks[:, :], blocks_i[:, :]))
            step(nc.vector.tensor_tensor_scan(ends[:, :], ones_bf[:, 0:E], blocks[:, :], 0.0, ALU.mult, ALU.add))
            step(nc.vector.tensor_tensor(base[:, :], ends[:, :], blocks[:, :], ALU.subtract))
            step(nc.vector.scalar_tensor_tensor(rank[:, :, :], base[:, :].unsqueeze(1).to_broadcast([P, NT, E]),
                                                float(P), rank[:, :, :], ALU.mult, ALU.add))
            step(nc.vector.tensor_tensor(onehot[:, :, :, :], onehot[:, :, :, :],
                                         rank[:, :, :].unsqueeze(1).to_broadcast([P, 2, NT, E]), ALU.mult))
            step(nc.vector.tensor_reduce(slot_f[:, :, :], onehot[:, :, :, :], AX.X, ALU.add))
            nc.vector.tensor_copy(slot_i[:, :, :], slot_f[:, :, :]).then_inc(slots_done, 1)
            step(nc.vector.tensor_tensor(past[:, :, :], ends[:, :].unsqueeze(1).to_broadcast([P, MAX_BLOCKS, E]),
                                         iota_b[:, :].unsqueeze(2).to_broadcast([P, MAX_BLOCKS, E]), ALU.is_le))
            step(nc.vector.tensor_reduce(block_e[:, :], past[:, :, :], AX.X, ALU.add))
            nc.vector.tensor_scalar(block_ei[:, :], block_e[:, :], float(E - 1), None, ALU.min).then_inc(slots_done, 1)
            dve.wait_ge(pexp_done, 1)
            step(nc.vector.tensor_scalar(wsel[:, 1, :], pexp[:, 1, :], 1.0, None, ALU.add))
            step(nc.vector.reciprocal(wsel[:, 0, :], wsel[:, 1, :]))
            step(nc.vector.tensor_scalar(wsel[:, 0, :], wsel[:, 0, :], tanh_g[:, 1:2], None, ALU.mult))
            nc.vector.tensor_tensor(wsel[:, 1, :], wsel[:, 0, :], pexp[:, 1, :], ALU.mult).then_inc(wsel_done, 1)

            shared_added(0)
            with dve.Fori(1, B) as i:
                shared_hidden(i, False)
                shared_added(i)

            def copy_xT(j, s, first=False):
                dve.wait_ge(bxT_ps, j + 1)
                if not first:
                    dve.wait_ge(bup_ps, 2 * j - 2)
                nc.vector.tensor_copy(blk_xT[:, s, :, :], bank(4)[:, 0:D].rearrange("p (c n) -> p c n", c=DC)
                                      ).then_inc(bxT_sb, 1)

            def hidden(j, s, first=False):
                dve.wait_ge(bsilu, j + 1)
                dve.wait_ge(bup_ps, 2 * j + 2)
                if not first:
                    dve.wait_ge(bhT_ps, j)
                nc.vector.tensor_tensor(blk_h[:, :], blk_gate[:, :], bank(2 * s + 1)[:, 0:HALF], ALU.mult
                                        ).then_inc(bhid, 1)

            def copy_y(j, s, first=False):
                dve.wait_ge(by_ps, j + 1)
                if not first:
                    dve.wait_ge(by_out[s], ((j - s) // 2 if isinstance(j, int) else j_half[0]) * 16)
                nc.vector.tensor_copy(blk_y[:, s, :], bank(6 + s)[:, 0:D]).then_inc(by_sb, 1)

            j_half = [None]
            copy_xT(0, 0, first=True)
            copy_xT(1, 1, first=True)
            hidden(0, 0, first=True)
            copy_xT(2, 0)
            hidden(1, 1)
            copy_y(0, 0, first=True)
            copy_xT(3, 1)
            hidden(2, 0)
            copy_y(1, 1, first=True)
            with dve.Fori(0, (MAX_BLOCKS - 5) // 2) as i:
                for q in range(2):
                    copy_xT(i * 2 + 4 + q, q)
                    hidden(i * 2 + 3 + q, (1 + q) % 2)
                    j_half[0] = i + 1
                    copy_y(i * 2 + 2 + q, q)
            for j in range(2 + 2 * ((MAX_BLOCKS - 5) // 2), MAX_BLOCKS):
                if j + 2 < MAX_BLOCKS:
                    copy_xT(j + 2, j % 2)
                if j + 1 < MAX_BLOCKS:
                    hidden(j + 1, (j + 1) % 2)
                copy_y(j, j % 2)

            for t in range(NT):
                dve.wait_ge(got_in[t % GB], 16 * TOPK * (t // GB + 1))
                nc.vector.scalar_tensor_tensor(x_sb[:, t, :], got[:, t % GB, 0, :], wsel[:, 0, t:t + 1], x_sb[:, t, :],
                                               ALU.mult, ALU.add).then_inc(x1_done, 1)
                dve.wait_ge(x1_done, NT + t + 1)
                nc.vector.scalar_tensor_tensor(x_sb[:, t, :], got[:, t % GB, 1, :], wsel[:, 1, t:t + 1], x_sb[:, t, :],
                                               ALU.mult, ALU.add).then_inc(added, 1)

        @block.tensor
        def _(pe):
            def mm(o_, w, m, start=True, stop=True):
                return nc.tensor.matmul(o_, w, m, start=start, stop=stop)

            pe.wait_ge(ident_done, 1)
            pe.wait_ge(w_attn_in, 16)
            for b in range(B):
                pe.wait_ge(ctx_in[b], 16)
                if b >= 1:
                    pe.wait_ge(resid_done, 2 * b - 1)
                for c in range(DC):
                    for d in range(DC):
                        last = mm(bank(4 + c), wkv_sb[:, d, c * P:(c + 1) * P], ctx_sb[:, d, b * T:(b + 1) * T],
                                  d == 0, d == DC - 1)
                last.then_inc(k_ps, 1)
                if b >= 1:
                    pe.wait_ge(v_done, b)
                for kt in range(TB):
                    for d in range(DC):
                        tok = b * T + kt * P
                        last = mm(bank(6 + kt // 2)[:, (kt % 2) * D:(kt % 2 + 1) * D], ctx_sb[:, d, tok:tok + P],
                                  wkv_sb[:, d, D:2 * D], d == 0, d == DC - 1)
                last.then_inc(v_ps, 1)
                pe.wait_ge(rows_done, b + 1)
                if b >= 1:
                    pe.wait_ge(rowsT_sb, b)
                for t in range(TB):
                    for c in range(DC):
                        last = nc.tensor.transpose(bank(c)[:, t * P:(t + 1) * P],
                                                   rows[:, b * TB + t, c * P:(c + 1) * P], ident[:, :])
                last.then_inc(rowsT_ps, 1)
                pe.wait_ge(rowsT_sb, b + 1)
                if b == 0:
                    pe.wait_ge(wq_in, 16)
                else:
                    pe.wait_ge(resid_done, 2 * b)
                for c in range(DC):
                    for d in range(DC):
                        last = mm(bank(2 + c), wq_sb[:, d, c * P:(c + 1) * P], xnT[:, d, b * T:(b + 1) * T],
                                  d == 0, d == DC - 1)
                last.then_inc(q_ps, 1)

            def max_tile(w, i, s, waits):
                p = i // 2
                if i % 2 == 0 and waits(p):
                    pe.wait_ge(max_done, 8 * w + p - 1)
                h, qt = i // TB, i % TB
                last = mm(bank(2 * (p % 2) + i % 2), q_unit[0:KROWS, s, h, qt * P:(qt + 1) * P],
                          k_unit[0:KROWS, s, h, :])
                if i % 2 == 1:
                    last.then_inc(pair_ps, 1)

            def turn_max(w, s):
                pe.wait_ge(max_done, 8 * w + 8)
                nc.tensor.transpose(bank(7)[:, 0:P], neg_max[:, s, :], ident[:, :]).then_inc(nmT_ps, 1)

            def pv(u, s, kt, half, first=False):
                if half == 0:
                    pe.wait_ge(exp_done, u * TB * HG + kt * HG + HG)
                    if kt == 0 and not first:
                        pe.wait_ge(o_done, u)
                cols = slice(half * T // 2, (half + 1) * T // 2)
                for h in range(HG):
                    last = nc.tensor.matmul(bank(6)[h * VW:(h + 1) * VW, cols], v_unit[:, s, kt, h * VW:(h + 1) * VW],
                                            probs[:, (kt * HG + h) % 8, cols], start=kt == 0 and half == 0,
                                            stop=kt == TB - 1, skip_group_check=True)
                if half == 1:
                    last.then_inc(pv_done, 1)

            def turn_out(u, s, qt):
                if qt == 0:
                    pe.wait_ge(o_done, u + 1)
                last = nc.tensor.transpose(bank(7)[:, qt * P:(qt + 1) * P], o_sb[:, s, qt * P:(qt + 1) * P], ident[:, :])
                if qt == TB - 1:
                    last.then_inc(oT_ps, 1)

            def slot(u, bu, r, first=False, more_max=True, more_turn=True):
                s, w = r % NG, (r + 2) % NG
                if more_max:
                    pe.wait_ge(unit_in[w], 16 * LOADS * (bu + (r + 2) // NG + 1))
                pe.wait_ge(nm_in[s], 16 * MROWS * (bu + r // NG + 1))
                for k in range(TB * HG):
                    kt, h = k // HG, k % HG
                    if not (first and k < 2):
                        pe.wait_ge(exp_done, u * TB * HG + k - 1)
                    mm(bank(4 + k % 2), k_unit[0:KROWS + MROWS, s, h, kt * P:(kt + 1) * P],
                       q_unit[0:KROWS + MROWS, s, h, :]).then_inc(score_ps, 1)
                    if more_max:
                        max_tile(u + 2, k, w, lambda p: True)
                    if k in (2, 3) and not first:
                        pv(u - 1, (r - 1) % NG, TB - 1, k - 2)
                    if k == TURN_MAX and more_turn:
                        if first:
                            pe.wait_ge(nmT_sb, 1)
                        else:
                            pe.wait_ge(attn_rows, u)
                        turn_max(u + 1, (r + 1) % 2)
                    if k in TURN_OUT and not first:
                        if k == TURN_OUT[0]:
                            if more_turn:
                                pe.wait_ge(nmT_sb, u + 2)
                            else:
                                pe.wait_ge(attn_rows, u)
                        turn_out(u - 1, (r - 1) % 2, k - TURN_OUT[0])
                    if kt >= 1 and k % 2 == 1:
                        pv(u, s, kt - 1, k % HG // 2, first)

            TURN_MAX, TURN_OUT = 1, (8, 9, 10, 11)

            pe.wait_ge(ones_rows, 1)
            pe.wait_ge(const_step, 3)
            pe.wait_ge(rowsT_sb, B)
            pe.wait_ge(resid_done, 2 * B)
            pe.wait_ge(v_done, B)
            for w in range(2):
                pe.wait_ge(unit_in[w], 16 * LOADS)
                for i in range(16):
                    max_tile(w, i, w, lambda p, w=w: w > 0 or p >= 2)
                if w == 0:
                    turn_max(0, 0)
            slot(0, 0, 0, first=True)
            with pe.Fori(0, B - 1) as b:
                for r in range(1, NG + 1):
                    slot(b * NG + r, b, r)
            for u in range(UNITS - 3, UNITS):
                slot(u, u // NG, u % NG, more_max=u + 2 < UNITS, more_turn=u + 1 < UNITS)
            for half in range(2):
                pv(UNITS - 1, (UNITS - 1) % NG, TB - 1, half)
            pe.wait_ge(attn_rows, UNITS)
            for qt in range(TB):
                turn_out(UNITS - 1, (UNITS - 1) % 2, qt)

            pe.wait_ge(small_in, 16 * 5)
            pe.wait_ge(attn_rows, UNITS + 1)

            def project(b):
                for t in range(b * TB, (b + 1) * TB + 1):
                    if t < (b + 1) * TB:
                        if t >= 2:
                            pe.wait_ge(atT_sb, t - 1)
                        for c in range(DC):
                            last = nc.tensor.transpose(bank(t % 2)[:, c * P:(c + 1) * P],
                                                       rows[:, t, c * P:(c + 1) * P], ident[:, :])
                        last.then_inc(atT_ps, 1)
                    if t > b * TB:
                        q = t - 1
                        pe.wait_ge(atT_sb, q + 1)
                        if q >= 2:
                            pe.wait_ge(x1_done, q - 1)
                        for c in range(DC):
                            last = mm(bank(3 + q % 2)[:, 0:D], attnT[:, q % 2, c, :], wp_sb[:, c, :],
                                      c == 0, c == DC - 1)
                        last.then_inc(proj_ps, 1)

            def turn_rows(b):
                pe.wait_ge(rows_done, B + b + 1)
                if b >= 1:
                    pe.wait_ge(rowsT_sb, B + b)
                for t in range(TB):
                    for c in range(DC):
                        last = nc.tensor.transpose(bank(2 + 3 * c)[:, t * P:(t + 1) * P],
                                                   rows[:, b * TB + t, c * P:(c + 1) * P], ident[:, :])
                last.then_inc(rowsT_ps, 1)

            def router(b):
                pe.wait_ge(rowsT_sb, B + b + 1)
                for t in range(b * TB, (b + 1) * TB):
                    for c in range(DC):
                        last = mm(bank(7)[:, t * E:(t + 1) * E], xnT[:, c, t * P:(t + 1) * P], gate_sb[:, c, :],
                                  c == 0, c == DC - 1)
                last.then_inc(logit_ps, 1)

            def shared_up(i, f, first):
                if not first:
                    pe.wait_ge(sh_hid, FC * i + f - FC + 1)
                    if f == 0:
                        pe.wait_ge(sh_added, 2 * i - 1)
                for half in range(2):
                    for c in range(DC):
                        col = half * HALF + f * P
                        last = mm(bank(3 * half + f), w_up[:, E, c, col:col + P], xnT[:, c, bass.ds(i * T, T)],
                                  c == 0, c == DC - 1)
                last.then_inc(sh_up_ps, 1)

            def shared_down(i, first):
                pe.wait_ge(sh_hid, FC * i + FC)
                for q in range(2):
                    if not first and q == 1:
                        pe.wait_ge(sh_added, 2 * i)
                    for t in range(2):
                        for f in range(FC):
                            tok = (2 * q + t) * P
                            last = mm(bank(6 * q)[:, t * D:(t + 1) * D], sh_hT[:, f, tok:tok + P], w_dn[:, E, f, :],
                                      f == 0, f == FC - 1)
                    last.then_inc(sh_y_ps, 1)

            project(0)
            project(1)
            turn_rows(0)
            project(2)
            router(0)
            turn_rows(1)
            project(3)
            router(1)
            turn_rows(2)
            pe.wait_ge(w_ffn_in, 16 * 2 * (E + 1))
            pe.wait_ge(x1_done, NT)
            shared_up(0, 0, True)
            router(2)
            shared_up(0, 1, True)
            turn_rows(3)
            router(3)
            pe.wait_ge(rowsT_sb, 2 * B)
            shared_up(0, 2, True)
            pe.wait_ge(chosen_done, 3)
            mm(bank(7)[:, 128:129], chosen[:, :, :].rearrange("p t e -> p (t e)"), ones_bf[:, 0:1]).then_inc(totals_ps, 1)
            shared_down(0, True)
            pe.wait_ge(totals_sb, 1)
            pe.wait_ge(const_step, 8)
            mm(bank(7)[:, 256:256 + NT * E], before[:, :], chosen[:, :, :].rearrange("p t e -> p (t e)"), True, False)
            mm(bank(7)[:, 256:256 + NT * E], totals[:, :], before_tile[:, :, :].rearrange("p t e -> p (t e)"),
               False, True)
            mm(bank(7)[:, 384:384 + E], totals[:, :], same_e_bf[:, :]).then_inc(rank_ps, 1)
            with pe.Fori(1, B) as i:
                for f in range(FC):
                    shared_up(i, f, False)
                shared_down(i, False)

            def expert(j):
                return pe.value_load(block_ei[0:1, bass.ds(j, 1)], min_val=0, max_val=E - 1)

            def turn_x(j, s, half, first=False):
                pe.wait_ge(bx_in[s], 16 * (half + 1))
                if not first:
                    pe.wait_ge(bxT_sb, j)
                for c in range(DC):
                    last = nc.tensor.transpose(bank(4)[:, c * P:(c + 1) * P], blk_x[:, s, c * P:(c + 1) * P],
                                               ident[:, :])
                last.then_inc(bxT_ps, 1)

            def up(j, s, first=False):
                e = expert(j)
                pe.wait_ge(bxT_sb, j + 1)
                if not first:
                    pe.wait_ge(bhid, j - 1)
                for g in range(2):
                    for c in range(DC):
                        last = mm(bank(2 * s + g)[:, 0:HALF], blk_xT[:, s, c, :],
                                  w_up[:, bass.ds(e, 1), c, g * HALF:(g + 1) * HALF].rearrange("p a f -> p (a f)"),
                                  c == 0, c == DC - 1)
                    last.then_inc(bup_ps, 1)

            def turn_h(j, first=False):
                pe.wait_ge(bhid, j + 1)
                if not first:
                    pe.wait_ge(bhT_sb, j)
                for f in range(FC):
                    last = nc.tensor.transpose(bank(5)[:, f * P:(f + 1) * P], blk_h[:, f * P:(f + 1) * P], ident[:, :])
                last.then_inc(bhT_ps, 1)

            def down(j, s, first=False):
                e = expert(j)
                pe.wait_ge(bhT_sb, j + 1)
                if not first:
                    pe.wait_ge(by_sb, j - 1)
                for f in range(FC):
                    last = mm(bank(6 + s)[:, 0:D], blk_hT[:, f, :],
                              w_dn[:, bass.ds(e, 1), f, :].rearrange("p a n -> p (a n)"), f == 0, f == FC - 1)
                last.then_inc(by_ps, 1)

            pe.wait_ge(slots_done, 2)
            pe.wait_ge(sh_added, 2 * B)
            turn_x(0, 0, 0, first=True)
            turn_x(1, 1, 0)
            up(0, 0, first=True)
            turn_h(0, first=True)
            turn_x(2, 0, 1)
            up(1, 1, first=True)
            down(0, 0, first=True)
            turn_h(1)
            turn_x(3, 1, 1)
            up(2, 0)
            down(1, 1, first=True)
            with pe.Fori(0, (MAX_BLOCKS - 5) // 2) as i:
                for q in range(2):
                    turn_h(i * 2 + 2 + q)
                    turn_x(i * 2 + 4 + q, q, i + 2)
                    up(i * 2 + 3 + q, (1 + q) % 2)
                    down(i * 2 + 2 + q, q)
            for j in range(2 + 2 * ((MAX_BLOCKS - 5) // 2), MAX_BLOCKS):
                turn_h(j)
                if j + 2 < MAX_BLOCKS:
                    turn_x(j + 2, j % 2, (j + 2) // 2)
                if j + 1 < MAX_BLOCKS:
                    up(j + 1, (j + 1) % 2)
                down(j, j % 2)


def kernel(x, ctx_1024, g_xattn, g_ffn, L0_xattn_W_kv, L0_xattn_W_q, L0_xattn_W_proj, L0_xattn_b_proj,
           L0_ffn_gate_w, L0_ffn_w_up, L0_ffn_w_down, L0_ffn_sg_gate, L0_ffn_sg_up, L0_ffn_sg_down):
    import concourse.bacc as bacc
    from concourse.bass_utils import run_bass_kernel_spmd

    def arr(a):
        return np.asarray(a)

    def by_unit(w):
        return w.reshape(D, NG, HG, HD).transpose(0, 1, 3, 2).reshape(D, D)

    shared_up = np.concatenate([arr(L0_ffn_sg_gate), arr(L0_ffn_sg_up)], axis=0)[None]
    host = {
        "x": arr(x),
        "ctxT": arr(ctx_1024).reshape(N, D).T,
        "g_xattn": arr(g_xattn),
        "g_ffn": arr(g_ffn),
        "w_kv": np.concatenate([by_unit(arr(L0_xattn_W_kv)[:, :D]), arr(L0_xattn_W_kv)[:, D:]], axis=1),
        "w_q": by_unit(arr(L0_xattn_W_q)),
        "w_proj": arr(L0_xattn_W_proj),
        "b_proj": arr(L0_xattn_b_proj),
        "gateT": arr(L0_ffn_gate_w).T,
        "w_upT": np.concatenate([arr(L0_ffn_w_up), shared_up], axis=0).transpose(0, 2, 1),
        "w_downT": np.concatenate([arr(L0_ffn_w_down), arr(L0_ffn_sg_down)[None]], axis=0).transpose(0, 2, 1),
    }
    host = {k: np.ascontiguousarray(v) for k, v in host.items()}
    nc = bacc.Bacc("TRN2", target_bir_lowering=False, num_devices=1)
    args = [nc.dram_tensor(f"in_{k}", v.shape, mybir.dt.from_np(v.dtype), kind="ExternalInput").ap()
            for k, v in host.items()]
    out = nc.dram_tensor("out", (B, T, D), F32, kind="ExternalOutput").ap()
    build(nc, *args, out)
    r = run_bass_kernel_spmd(nc, [{f"in_{k}": v for k, v in host.items()}], core_ids=[0])
    return r.results[0]["out"]
```

```python
from contextlib import ExitStack

import concourse.bass as bass
import numpy as np
from concourse import mybir

P = 128
F32, BF16, I32, U32 = mybir.dt.float32, mybir.dt.bfloat16, mybir.dt.int32, mybir.dt.uint32
ALU = mybir.AluOpType
ACT = mybir.ActivationFunctionType
AX = mybir.AxisListType

B, T, D = 4, 512, 256
N = B * T
NT = N // P
TB = T // P
DC = D // P
H, HD = 16, 16
HG = 4
NG = H // HG
UNITS = B * NG
VW = 32
E, HALF, FFN = 8, 384, 768
FC = HALF // P
TOPK = 2
MAX_BLOCKS = (TOPK * N + E * (P - 1)) // P
EPS = 1e-5
K_RUNS = ((0, 1, 2), (0,), (0, 1))
Q_RUNS = ((0, 1), (0, 1, 2), (0,))
PROJECT_AT = (0, 2, 4, 6, 12, 14)
assert 2 * len(PROJECT_AT) == NT - TB
QK_ORDER = [(a, b) for b in range(B) for a in (0, 1)]
OUTS = 2 * (H // 4) + 1
K_PARTS, Q_PARTS = sum(K_RUNS, ()), sum(Q_RUNS, ())
assert sorted(zip(K_PARTS, Q_PARTS)) == [(i, j) for i in range(3) for j in range(3 - i)]
KROWS = len(K_PARTS) * HD
MROWS = 3
LOADS = len(K_RUNS) + len(Q_RUNS) + 1
TOKEN, WEIGHT, SLOT = D, D + 1, D + 2
OUT_ROWS = N + P


def build(nc, x, ctxT, g_xattn, g_ffn, w_kv, w_q, w_proj, b_proj, gateT, w_upT, w_downT, out):
    qk_parts = nc.dram_tensor("qk_parts", (2, B, NG, 3, HD * HG, T), BF16, kind="Internal").ap()
    v_rows = nc.dram_tensor("v_rows", (B, P, TB, H * VW), F32, kind="Internal").ap()
    x_slots = nc.dram_tensor("x_slots", (MAX_BLOCKS * P, SLOT), F32, kind="Internal").ap()

    x_dram = x.rearrange("b (t p) d -> p (b t) d", p=P)
    out_dram = out[0:N, :].rearrange("(t p) d -> p t d", p=P)

    with ExitStack() as ctx:
        def sb(name, shape, dt=F32):
            return ctx.enter_context(nc.sbuf_tensor(name, shape, dt))

        def sem(name):
            return ctx.enter_context(nc.semaphore(name))

        x_sb = sb("x_sb", [P, NT, D])
        slot_rows = sb("slot_rows", [P, NT, SLOT])
        rows = slot_rows[:, :, 0:D]
        xnT = sb("xnT", [P, DC, N])
        ctx_region = sb("ctx_region", [P, DC * N])
        ctx_sb = ctx_region[:, :].rearrange("p (c n) -> p c n", c=DC)
        probs = ctx_region[:, :].rearrange("p (s n) -> p s n", n=T)
        up_region = sb("up_region", [P, (E + 1) * DC * FFN])
        w_up = up_region[:, :].rearrange("p (e c f) -> p e c f", e=E + 1, c=DC)
        dn_region = sb("dn_region", [P, (E + 1) * FC * D])
        w_dn = dn_region[:, :].rearrange("p (e f n) -> p e f n", e=E + 1, f=FC)
        part_words = B * 2 * 3 * DC * T // 2
        parts = up_region[:, 0:part_words].bitcast(BF16).rearrange("p (b a j c n) -> p b a j c n", b=B, a=2, j=3, c=DC)
        resid = dn_region[:, 0:2 * DC * T].rearrange("p (a c n) -> p a c n", a=2, c=DC)
        v_sb = dn_region[:, 2 * DC * T:2 * DC * T + 2 * TB * H * VW].rearrange(
            "p (s k h w) -> p s k h w", s=2, k=TB, h=H)

        unit_words = 2 * 4 * HG * T // 2 + 4 * TB * HG * VW
        unit_region = sb("unit_region", [P, unit_words])
        k_unit = unit_region[:, 0:4 * HG * T // 2].bitcast(BF16).rearrange("p (s h n) -> p s h n", s=4, h=HG)
        q_unit = unit_region[:, 4 * HG * T // 2:4 * HG * T].bitcast(BF16).rearrange(
            "p (s h n) -> p s h n", s=4, h=HG)
        v_unit = unit_region[:, 4 * HG * T:unit_words].rearrange("p (s k c) -> p s k c", s=4, k=TB)
        attnT = xnT[:, :, N - T:N].rearrange("p c (s n) -> p s c n", s=TB)
        used = [0]

        def work(words, pattern, **sizes):
            a = used[0]
            used[0] += words
            assert used[0] <= unit_words
            return unit_region[:, a:a + words].rearrange(pattern, **sizes)

        sh_gate = work(FC * T, "p (f n) -> p f n", f=FC)
        sh_hT = work(FC * T, "p (f n) -> p f n", f=FC)
        blk_x = work(2 * SLOT, "p (s d) -> p s d", s=2)
        blk_xT = work(2 * D, "p (s c n) -> p s c n", s=2, c=DC)
        blk_gate = work(HALF, "p f -> p f")
        blk_h = work(HALF, "p f -> p f")
        blk_hT = work(HALF, "p (f n) -> p f n", f=FC)
        blk_y = work(2 * D, "p (s d) -> p s d", s=2)
        logits = work(NT * E, "p (t e) -> p t e", t=NT)
        top8 = work(NT * 8, "p (t e) -> p t e", t=NT)
        onehot = work(2 * NT * E, "p (k t e) -> p k t e", k=2, t=NT)
        rank = work(NT * E, "p (t e) -> p t e", t=NT)
        past = work(MAX_BLOCKS * E, "p (j e) -> p j e", e=E)
        blk_row = work(MAX_BLOCKS, "p j -> p j").bitcast(I32)
        blk_weight = work(MAX_BLOCKS, "p j -> p j")

        wq_sb = sb("wq_sb", [P, DC, D])
        wkv_sb = sb("wkv_sb", [P, DC, 2 * D])
        wp_sb = sb("wp_sb", [P, DC, D])
        gate_sb = sb("gate_sb", [P, DC, E])
        bias_sb = sb("bias_sb", [P, D])
        gates = sb("gates", [P, 2])
        tanh_g = sb("tanh_g", [P, 2])
        eps_sb = sb("eps_sb", [P, 1])
        ident = sb("ident", [P, P])
        stats = sb("stats", [P, NT, 6])
        mean_var = sb("mean_var", [P, NT, 2])
        std = sb("std", [P, NT])
        rstd = sb("rstd", [P, NT])
        neg_max = sb("neg_max", [P, 2, P])
        nmT = sb("nmT", [HG * TB, P])
        nm_res = sb("nm_res", [HG * TB, P])
        nm_parts = sb("nm_parts", [HG * TB, 3, P], BF16)
        o_sb = sb("o_sb", [P, 2, T])
        rinv = sb("rinv", [P, TB, HG])
        empty = sb("empty", [P, SLOT])
        ones_bf = sb("ones_bf", [P, P], BF16)
        before = sb("before", [P, P], BF16)
        before_tile = sb("before_tile", [P, NT, E], BF16)
        same_e = sb("same_e", [P, E])
        same_e_bf = sb("same_e_bf", [P, E], BF16)
        iota_e = sb("iota_e", [P, E])
        iota_b = sb("iota_b", [P, MAX_BLOCKS])
        top8_idx = sb("top8_idx", [P, NT, 8], U32)
        topi = sb("topi", [P, 2, NT])
        chosen = sb("chosen", [P, NT, E], BF16)
        totals = sb("totals", [P, P], BF16)
        count = sb("count", [P, E])
        count_i = sb("count_i", [P, E], I32)
        blocks_i = sb("blocks_i", [P, E], I32)
        blocks = sb("blocks", [P, E])
        ends = sb("ends", [P, E])
        base = sb("base", [P, E])
        block_e = sb("block_e", [P, MAX_BLOCKS])
        block_ei = sb("block_ei", [P, MAX_BLOCKS], I32)
        token_f = sb("token_f", [P, NT])
        slot_f = sb("slot_f", [P, 2, NT])
        slot_i = sb("slot_i", [P, 2, NT], I32)
        pexp = sb("pexp", [P, 2, NT])
        wsel = sb("wsel", [P, 2, NT])

        ps = [ctx.enter_context(nc.psum_tensor(f"ps{i}", [P, 4, 512], F32)) for i in range(2)]

        def bank(i, n=1):
            return ps[i // 4][:, i % 4, :] if n == 1 else ps[i // 4][:, i % 4:i % 4 + n, :]

        def turned(t):
            return bank(t % 2 if t < NT - TB else (0, 1, 6, 7)[t % TB])[:, 0:D]

        def projected(t):
            return bank(2 + t % 2 if t < NT - TB else (4, 3, 2, 5)[t % TB])[:, 0:D]

        def rowsT_bank(b, c):
            return bank(((0, 6), (1, 4))[b % 2][c])

        x_in = [sem(f"x_in{b}") for b in range(B)]
        ctx_in = [sem(f"ctx_in{b}") for b in range(B)]
        wkv_in, wq_in = sem("wkv_in"), sem("wq_in")
        gates_in = sem("gates_in")
        small_in = sem("small_in")
        const_step = sem("const_step")
        ident_done = sem("ident_done")
        tanh_done = sem("tanh_done")
        bias_done = sem("bias_done")
        ones_rows = sem("ones_rows")
        v_ones = sem("v_ones")
        resid_base = sem("resid_base")
        stat_done = sem("stat_done")
        var_done = sem("var_done")
        std_done = sem("std_done")
        rstd_done = sem("rstd_done")
        rows_done = sem("rows_done")
        rowsT_ps = sem("rowsT_ps")
        rowsT_sb = sem("rowsT_sb")
        k_ps, v_ps, q_ps = sem("k_ps"), sem("v_ps"), sem("q_ps")
        high_done = sem("high_done")
        resid_done = sem("resid_done")
        v_done = sem("v_done")
        mid_done = sem("mid_done")
        low_done = sem("low_done")
        qkv_out = [sem(f"qkv_out{b}") for b in range(B)]
        unit_in = [sem(f"unit_in{s}") for s in range(4)]
        pair_ps = sem("pair_ps")
        max_done = sem("max_done")
        nmT_ps, nmT_sb = sem("nmT_ps"), sem("nmT_sb")
        nm_step = sem("nm_step")
        nm_split = sem("nm_split")
        nm_in = [sem(f"nm_in{s}") for s in range(4)]
        score_ps = sem("score_ps")
        exp_done = sem("exp_done")
        pv_done = sem("pv_done")
        o_done = sem("o_done")
        oT_ps = sem("oT_ps")
        rinv_done = sem("rinv_done")
        attn_rows = sem("attn_rows")
        w_ffn_in = sem("w_ffn_in")
        zero_out = sem("zero_out")
        atT_ps, atT_sb = sem("atT_ps"), sem("atT_sb")
        proj_ps = sem("proj_ps")
        x1_done = sem("x1_done")
        logit_ps = sem("logit_ps")
        route = sem("route")
        chosen_done = sem("chosen_done")
        totals_ps, totals_sb = sem("totals_ps"), sem("totals_sb")
        rank_ps = sem("rank_ps")
        pexp_done = sem("pexp_done")
        slots_done = sem("slots_done")
        weight_set = sem("weight_set")
        scattered = sem("scattered")
        sh_up_ps = sem("sh_up_ps")
        sh_silu = sem("sh_silu")
        sh_hid = sem("sh_hid")
        sh_y_ps = sem("sh_y_ps")
        sh_added = sem("sh_added")
        bx_in = [sem(f"bx_in{s}") for s in range(2)]
        bxT_ps, bxT_sb = sem("bxT_ps"), sem("bxT_sb")
        bup_ps = sem("bup_ps")
        bsilu = sem("bsilu")
        bhid = sem("bhid")
        bhT_ps, bhT_sb = sem("bhT_ps"), sem("bhT_sb")
        by_ps, by_sb = sem("by_ps"), sem("by_sb")
        by_out = [sem(f"by_out{s}") for s in range(2)]
        token_read = sem("token_read")
        out_done = sem("out_done")

        block = ctx.enter_context(nc.Block())

        @block.sync
        def _(sp):
            for b in range(B):
                sp.dma_start(x_sb[:, b * TB:(b + 1) * TB, :], x_dram[:, b * TB:(b + 1) * TB, :]).then_inc(x_in[b], 16)
                if b == 0:
                    sp.dma_start(wq_sb[:, :, :], w_q.rearrange("(c p) n -> p c n", p=P)).then_inc(wq_in, 16)
                    sp.dma_start(wkv_sb[:, :, :], w_kv.rearrange("(c p) n -> p c n", p=P)).then_inc(wkv_in, 16)
                sp.dma_start(ctx_sb[:, :, b * T:(b + 1) * T],
                             ctxT.rearrange("(c p) n -> p c n", p=P)[:, :, b * T:(b + 1) * T]).then_inc(ctx_in[b], 16)

            def load_unit(b, g):
                for a, dst, runs in ((1, k_unit, K_RUNS), (0, q_unit, Q_RUNS)):
                    row = 0
                    for run in runs:
                        n = len(run)
                        src = qk_parts[a, bass.ds(b, 1), g, 0:n, :, :].rearrange("a j (d h) n -> (a j d) (h n)", h=HG)
                        to = dst[row:row + n * HD, g, :, :].rearrange("p h n -> p (h n)")
                        sp.dma_start(to, src).then_inc(unit_in[g], 16)
                        row += n * HD
                src = v_rows[bass.ds(b, 1), :, :, g * HG * VW:(g + 1) * HG * VW].rearrange("a p k c -> p (a k) c")
                sp.dma_start(v_unit[:, g, :, :], src).then_inc(unit_in[g], 16)

            for n, (a, b) in enumerate(QK_ORDER):
                sp.wait_ge(low_done, n + 1)
                for g in range(NG):
                    half = P // 2 * (g % 2)
                    sp.dma_start(qk_parts[a, b, g, :, :, :].rearrange("j r n -> r j n"),
                                 parts[half:half + P // 2, b, a, :, g // 2, :]).then_inc(qkv_out[b], 16)
                if a == 1:
                    sp.wait_ge(v_done, b + 1)
                    sp.dma_start(v_rows[b, :, :, :], v_sb[:, b % 2, :, :, :].rearrange("p k h w -> p k (h w)")
                                 ).then_inc(qkv_out[b], 16)
                if (a, b) == (1, 1):
                    sp.wait_ge(qkv_out[0], 16 * OUTS)
                    for g in range(NG):
                        load_unit(0, g)
            def send_max(u, g):
                sp.wait_ge(nm_split, u + 1)
                for j in range(MROWS):
                    dst = q_unit[KROWS + j:KROWS + j + 1, g, :, :].rearrange("a h (t n) -> a (h t) n", n=P)
                    sp.dma_start(dst, nm_parts[:, j, :]).then_inc(nm_in[g], 16)

            send_max(0, 0)
            for b in range(1, B):
                sp.wait_ge(qkv_out[b], 16 * OUTS)
            with sp.Fori(0, B - 1) as b:
                for g in range(NG):
                    send_max(b * NG + g + 1, (g + 1) % NG)
                    sp.wait_ge(pv_done, (b * NG + g) * TB + TB)
                    load_unit(b + 1, g)
            for u in range(UNITS - 3, UNITS):
                send_max(u, u % NG)

            sp.dma_start(out[N:OUT_ROWS, :], empty[:, 0:D]).then_inc(out_done, 16)

            def store_base(b):
                sp.wait_ge(sh_added, 2 * b + 2)
                sp.dma_start(out_dram[:, b * TB:(b + 1) * TB, :], x_sb[:, b * TB:(b + 1) * TB, :]).then_inc(out_done, 16)

            for b in range(B - 1):
                store_base(b)

            def load_block(j, s):
                sp.dma_start(blk_x[:, s, :], x_slots[bass.ds(j * P, P), :]).then_inc(bx_in[s], 16)

            sp.wait_ge(zero_out, 16)
            sp.wait_ge(scattered, 16 * 2 * NT)
            load_block(0, 0)
            load_block(1, 1)
            store_base(B - 1)
            for j in (2, 3):
                sp.wait_ge(token_read, j - 1)
                load_block(j, j % 2)
            PAIRS = (MAX_BLOCKS - 4) // 2
            with sp.Fori(0, PAIRS) as i:
                for q in range(2):
                    sp.wait_ge(token_read, i * 2 + q + 3)
                    load_block(i * 2 + q + 4, q)
            for j in range(4 + 2 * PAIRS, MAX_BLOCKS):
                sp.wait_ge(token_read, j - 1)
                load_block(j, j % 2)
            sp.wait_ge(out_done, 16 * (B + 1))
            for s in range(2):
                sp.wait_ge(by_out[s], 16 * ((MAX_BLOCKS + 1 - s) // 2))

        @block.gpsimd
        def _(pool):
            nc.gpsimd.memset(ident[:, :], 0.0).then_inc(const_step, 1)
            pool.wait_ge(const_step, 1)
            nc.gpsimd.affine_select(out=ident[:, :], in_=ident[:, :], compare_op=ALU.not_equal, fill=1.0, base=0,
                                    pattern=[[-1, P]], channel_multiplier=1).then_inc(ident_done, 1)
            pool.wait_ge(ident_done, 1)
            nc.gpsimd.memset(empty[:, :], 0.0).then_inc(const_step, 1)
            pool.wait_ge(const_step, 2)
            nc.gpsimd.memset(neg_max[:, :, :], 0.0).then_inc(const_step, 1)
            pool.wait_ge(const_step, 3)
            nc.gpsimd.memset(ones_bf[:, :], 1.0).then_inc(const_step, 1)
            pool.wait_ge(const_step, 4)
            nc.gpsimd.affine_select(out=before[:, :], in_=ones_bf[:, :], compare_op=ALU.is_gt, fill=0.0, base=0,
                                    pattern=[[1, P]], channel_multiplier=-1).then_inc(const_step, 1)
            pool.wait_ge(const_step, 5)
            nc.gpsimd.iota(iota_e[:, :], pattern=[[1, E]], base=0, channel_multiplier=0,
                           allow_small_or_imprecise_dtypes=True).then_inc(const_step, 1)
            pool.wait_ge(const_step, 6)
            nc.gpsimd.iota(iota_b[:, :], pattern=[[1, MAX_BLOCKS]], base=0, channel_multiplier=0,
                           allow_small_or_imprecise_dtypes=True).then_inc(const_step, 1)
            pool.wait_ge(const_step, 7)
            nc.gpsimd.iota(empty[:, TOKEN:TOKEN + 1], pattern=[[0, 1]], base=N, channel_multiplier=1,
                           allow_small_or_imprecise_dtypes=True).then_inc(const_step, 1)
            pool.wait_ge(const_step, 8)
            nc.gpsimd.iota(token_f[:, :], pattern=[[P, NT]], base=0, channel_multiplier=1,
                           allow_small_or_imprecise_dtypes=True).then_inc(const_step, 1)
            pool.wait_ge(const_step, 9)
            nc.gpsimd.memset(v_sb[:, :, :, :, HD:VW], 1.0).then_inc(v_ones, 1)
            pool.wait_ge(v_ones, 1)
            nc.gpsimd.memset(k_unit[KROWS:KROWS + MROWS, :, :, :], 1.0).then_inc(ones_rows, 1)
            pool.wait_ge(ones_rows, 1)
            pool.wait_ge(route, 2)
            nc.gpsimd.affine_select(out=before_tile[:, :, :], in_=before_tile[:, :, :], compare_op=ALU.is_gt,
                                    fill=0.0, base=0, pattern=[[E, NT], [1, E]], channel_multiplier=-1
                                    ).then_inc(const_step, 1)
            pool.wait_ge(const_step, 10)
            pool.wait_ge(bias_done, 1)
            for t in range(NT):
                pool.wait_ge(rows_done, t // TB + 1)
                nc.gpsimd.tensor_tensor(x_sb[:, t, :], x_sb[:, t, :], bias_sb[:, :], ALU.add).then_inc(resid_base, 1)
            pool.wait_ge(resid_base, NT)

            def split_max(u):
                pool.wait_ge(nmT_sb, u + 1)
                if u >= 1:
                    pool.wait_ge(nm_in[(u - 1) % NG], 16 * MROWS * ((u - 1) // NG + 1))
                nc.gpsimd.tensor_copy(nm_parts[:, 0, :], nmT[:, :]).then_inc(nm_step, 1)
                pool.wait_ge(nm_step, 3 * u + 1)
                nc.gpsimd.tensor_tensor(nm_res[:, :], nmT[:, :], nm_parts[:, 0, :], ALU.subtract).then_inc(nm_step, 1)
                pool.wait_ge(nm_step, 3 * u + 2)
                nc.gpsimd.tensor_copy(nm_parts[:, 1, :], nm_res[:, :]).then_inc(nm_step, 1)
                pool.wait_ge(nm_step, 3 * u + 3)
                nc.gpsimd.tensor_tensor(nm_parts[:, 2, :], nm_res[:, :], nm_parts[:, 1, :], ALU.subtract
                                        ).then_inc(nm_split, 1)
                pool.wait_ge(nm_split, u + 1)

            for u in range(UNITS):
                split_max(u)

            pool.wait_ge(slots_done, 1)
            pool.wait_ge(zero_out, 16)
            for k in range(TOPK):
                if k >= 1:
                    pool.wait_ge(scattered, 16 * NT * k)
                    nc.gpsimd.tensor_copy(slot_rows[:, :, WEIGHT], wsel[:, k, :]).then_inc(weight_set, 1)
                pool.wait_ge(weight_set, k + 1)
                for t in range(NT):
                    pool.indirect_dma_start(
                        out=x_slots[:, :], out_offset=bass.IndirectOffsetOnAxis(ap=slot_i[:, k, t:t + 1], axis=0),
                        in_=slot_rows[:, t, :], in_offset=None).then_inc(scattered, 16)
            pool.wait_ge(out_done, 16 * (B + 1))
            for j in range(MAX_BLOCKS):
                pool.wait_ge(by_sb, j + 1)
                if j >= 1:
                    pool.wait_ge(by_out[(j - 1) % 2], 16 * ((j - 1) // 2 + 1))
                pool.indirect_dma_start(
                    out=out[:, :], out_offset=bass.IndirectOffsetOnAxis(ap=blk_row[:, j:j + 1], axis=0),
                    in_=blk_y[:, j % 2, :], in_offset=None, compute_op=ALU.add).then_inc(by_out[j % 2], 16)

        @block.scalar
        def _(act):
            act.dma_start(gates[:, 0:1], g_xattn.partition_broadcast(P)).then_inc(gates_in, 16)
            act.dma_start(gates[:, 1:2], g_ffn.partition_broadcast(P)).then_inc(gates_in, 16)
            act.wait_ge(gates_in, 16 * 2)
            nc.scalar.activation(tanh_g[:, :], gates[:, :], ACT.Tanh).then_inc(tanh_done, 1)

            def std_of(b, n):
                act.wait_ge(var_done, n)
                nc.scalar.activation(std[:, b * TB:(b + 1) * TB], mean_var[:, b * TB:(b + 1) * TB, 1], ACT.Sqrt,
                                     bias=eps_sb[:, 0:1]).then_inc(std_done, 1)

            def mid_part(n):
                a, b = QK_ORDER[n]
                act.wait_ge(resid_done, n + 1)
                nc.scalar.copy(parts[:, b, a, 1, :, :], resid[:, a, :, :]).then_inc(mid_done, 1)

            def copy_xnT(b):
                act.wait_ge(rowsT_ps, b + 1)
                nc.scalar.copy(xnT[:, :, b * T:(b + 1) * T], bank(0, 2)).then_inc(rowsT_sb, 1)

            std_of(0, 1)
            act.dma_start(bias_sb[:, :], b_proj.partition_broadcast(P)).then_inc(small_in, 16)
            act.dma_start(wp_sb[:, :, :], w_proj.rearrange("(c p) n -> p c n", p=P)).then_inc(small_in, 16)
            act.dma_start(gate_sb[:, :, :], gateT.rearrange("(c p) n -> p c n", p=P)).then_inc(small_in, 16)
            copy_xnT(0)
            for b in range(B):
                act.wait_ge(q_ps, b + 1)
                nc.scalar.mul(parts[:, b, 0, 0, :, :], bank(2, 2), float(HD) ** -0.5).then_inc(high_done, 1)
                if b + 1 < B:
                    std_of(b + 1, b + 2)
                if b >= 1:
                    mid_part(2 * b - 1)
                act.wait_ge(k_ps, b + 1)
                nc.scalar.copy(parts[:, b, 1, 0, :, :], bank(4, 2)).then_inc(high_done, 1)
                mid_part(2 * b)
                if b + 1 < B:
                    copy_xnT(b + 1)
                act.wait_ge(v_ps, b + 1)
                if b == 0:
                    act.wait_ge(v_ones, 1)
                if b >= 2:
                    act.wait_ge(qkv_out[b - 2], 16 * OUTS)
                nc.scalar.copy(v_sb[:, b % 2, :, :, 0:HD],
                               bank(6, 2).rearrange("p a (k h w) -> p (a k) h w", k=2, h=H)).then_inc(v_done, 1)
            mid_part(2 * B - 1)
            act.wait_ge(const_step, 8)

            def load_expert(e):
                act.dma_start(w_up[:, bass.ds(e, 1), :, :].rearrange("p a c f -> p (a c) f"),
                              w_upT[bass.ds(e, 1), :, :].rearrange("a (c p) f -> p (a c) f", p=P)).then_inc(w_ffn_in, 16)
                act.dma_start(w_dn[:, bass.ds(e, 1), :, :].rearrange("p a c n -> p (a c) n"),
                              w_downT[bass.ds(e, 1), :, :].rearrange("a (c p) n -> p (a c) n", p=P)
                              ).then_inc(w_ffn_in, 16)

            def copy_max(u, first=False):
                if not first:
                    act.wait_ge(nm_split, u)
                act.wait_ge(nmT_ps, u + 1)
                nc.scalar.copy(nmT[:, :], bank(7)[0:HG * TB, 0:P]).then_inc(nmT_sb, 1)

            def copy_out(u, s):
                act.wait_ge(pv_done, u * TB + TB)
                nc.scalar.copy(o_sb[:, s, :], bank(6)).then_inc(o_done, 1)

            def exp_slot(u, g, first=False, more_max=True):
                for k in range(TB * HG):
                    kt = k // HG
                    if k % HG == 0 and not (first and kt < 2):
                        act.wait_ge(pv_done, u * TB + kt - 1)
                    act.wait_ge(score_ps, u * TB * HG + k + 1)
                    nc.scalar.activation(probs[:, k % 8, :], bank(4 + k % 2), ACT.Exp).then_inc(exp_done, 1)
                    if k == 3 and not first:
                        copy_out(u - 1, (g + 1) % 2)
                    if k == 4 and more_max:
                        copy_max(u + 1)

            copy_max(0, first=True)
            exp_slot(0, 0, first=True)
            for b in range(B):
                act.wait_ge(qkv_out[b], 16 * OUTS)
            with act.Fori(0, B - 1) as b:
                for r in range(1, NG + 1):
                    if r < NG:
                        load_expert(b * 3 + r - 1)
                    exp_slot(b * NG + r, r % NG)
            act.dma_start(x_slots.rearrange("(j p) d -> p j d", p=P),
                          empty[:, :].unsqueeze(1).to_broadcast([P, MAX_BLOCKS, SLOT])).then_inc(zero_out, 16)
            for u in range(UNITS - 3, UNITS):
                exp_slot(u, u % NG, more_max=u + 1 < UNITS)
            copy_out(UNITS - 1, (UNITS - 1) % 2)

            def copy_rowsT(b):
                act.wait_ge(rowsT_ps, B + b + 1)
                for c in range(DC):
                    last = nc.scalar.copy(xnT[:, c, b * T:(b + 1) * T], rowsT_bank(b, c))
                last.then_inc(rowsT_sb, 1)

            std_of(0, B + 1)
            std_of(1, B + 2)
            for t in range(NT - TB, NT):
                act.wait_ge(atT_ps, t + 1)
                nc.scalar.copy(attnT[:, t % TB, :, :], turned(t).rearrange("p (c n) -> p c n", c=DC)).then_inc(atT_sb, 1)
            std_of(2, B + 3)
            copy_rowsT(0)
            copy_rowsT(1)
            std_of(3, B + 4)
            copy_rowsT(2)
            copy_rowsT(3)
            act.wait_ge(route, 3)
            nc.scalar.activation(pexp[:, 1, :], pexp[:, 0, :], ACT.Exp).then_inc(pexp_done, 1)

            def shared_silu(i, f, first=False):
                act.wait_ge(sh_up_ps, FC * i + f + 1)
                if not first:
                    act.wait_ge(sh_hid, FC * i + f - FC + 1)
                nc.scalar.activation(sh_gate[:, f, :], bank(f), ACT.Silu).then_inc(sh_silu, 1)

            for f in range(FC):
                shared_silu(0, f, first=True)
            with act.Fori(1, B) as i:
                for f in range(FC):
                    shared_silu(i, f)

            def block_silu(j, s, first=False):
                act.wait_ge(bup_ps, 2 * j + 1)
                if not first:
                    act.wait_ge(bhid, j)
                nc.scalar.activation(blk_gate[:, :], bank(2 * s)[:, 0:HALF], ACT.Silu).then_inc(bsilu, 1)

            def block_hT(j, first=False):
                act.wait_ge(bhT_ps, j + 1)
                if not first:
                    act.wait_ge(by_ps, j)
                nc.scalar.copy(blk_hT[:, :, :], bank(5)[:, 0:HALF].rearrange("p (f n) -> p f n", f=FC)
                               ).then_inc(bhT_sb, 1)

            block_silu(0, 0, first=True)
            block_hT(0, first=True)
            block_silu(1, 1)
            with act.Fori(0, (MAX_BLOCKS - 3) // 2) as i:
                for q in range(2):
                    block_hT(i * 2 + 1 + q)
                    block_silu(i * 2 + 2 + q, q)
            block_hT(MAX_BLOCKS - 2)
            block_silu(MAX_BLOCKS - 1, (MAX_BLOCKS - 1) % 2)
            block_hT(MAX_BLOCKS - 1)

        @block.vector
        def _(dve):
            nc.vector.memset(eps_sb[:, :], EPS)
            dve.sem_inc(attn_rows, 1)

            def ln_stats(b, n):
                for t in range(b * TB, (b + 1) * TB):
                    last = nc.vector.bn_stats(stats[:, t, :], x_sb[:, t, :])
                last.then_inc(stat_done, 1)
                dve.wait_ge(stat_done, n)
                for t in range(b * TB, (b + 1) * TB):
                    last = nc.vector.bn_aggr(mean_var[:, t, :], stats[:, t, :])
                last.then_inc(var_done, 1)

            def ln_apply(b, n):
                dve.wait_ge(std_done, n)
                nc.vector.reciprocal(rstd[:, b * TB:(b + 1) * TB], std[:, b * TB:(b + 1) * TB]).then_inc(rstd_done, 1)
                dve.wait_ge(rstd_done, n)
                for t in range(b * TB, (b + 1) * TB):
                    last = nc.vector.tensor_scalar(rows[:, t, :], x_sb[:, t, :], mean_var[:, t, 0:1],
                                                   rstd[:, t:t + 1], ALU.subtract, ALU.mult)
                last.then_inc(rows_done, 1)

            for b in range(2):
                dve.wait_ge(x_in[b], 16)
                ln_stats(b, b + 1)
                if b == 0:
                    ln_apply(0, 1)

            def low_part(i):
                a, b = QK_ORDER[i]
                dve.wait_ge(mid_done, i + 1)
                nc.vector.tensor_tensor(parts[:, b, a, 2, :, :], resid[:, a, :, :], parts[:, b, a, 1, :, :],
                                        ALU.subtract).then_inc(low_done, 1)

            for n, (a, b) in enumerate(QK_ORDER, 1):
                first_bank, scale = ((2, float(HD) ** -0.5), (4, 1.0))[a]
                dve.wait_ge(high_done, n)
                if n >= 3:
                    dve.wait_ge(low_done, n - 2)
                for c in range(DC):
                    last = nc.vector.scalar_tensor_tensor(resid[:, a, c, :], bank(first_bank + c), scale,
                                                          parts[:, b, a, 0, c, :], ALU.mult, ALU.subtract)
                last.then_inc(resid_done, 1)
                if a == 0 and b + 1 < B:
                    ln_apply(b + 1, b + 2)
                if n >= 2:
                    low_part(n - 2)
                if a == 1 and b + 2 < B:
                    dve.wait_ge(x_in[b + 2], 16)
                    ln_stats(b + 2, b + 3)
                if n == 2:
                    dve.wait_ge(tanh_done, 1)
                    dve.wait_ge(small_in, 16 * 3)
                    nc.vector.tensor_scalar(bias_sb[:, :], bias_sb[:, :], tanh_g[:, 0:1], None, ALU.mult
                                            ).then_inc(bias_done, 1)
                    dve.wait_ge(ident_done, 1)
                    nc.vector.tensor_reduce(same_e[:, :], ident[:, :].rearrange("p (t e) -> p e t", e=E), AX.X,
                                            ALU.add).then_inc(route, 1)
                    dve.wait_ge(route, 1)
                    nc.vector.tensor_copy(same_e_bf[:, :], same_e[:, :])
                    nc.vector.tensor_copy(before_tile[:, :, :],
                                          same_e[:, :].unsqueeze(1).to_broadcast([P, NT, E])).then_inc(route, 1)
            low_part(2 * B - 1)

            def max_pair(w, p, s):
                dve.wait_ge(pair_ps, 8 * w + p + 1)
                nc.vector.tensor_reduce(neg_max[:, s, 2 * p:2 * p + 2], bank(2 * (p % 2), 2), AX.X, ALU.max,
                                        negate=True).then_inc(max_done, 1)

            def normalise(u, b, g):
                dve.wait_ge(oT_ps, u + 1)
                o4 = bank(7).rearrange("p (t h w) -> p t h w", t=TB, h=HG)
                nc.vector.reciprocal(rinv[:, :, :], o4[:, :, :, HD]).then_inc(rinv_done, 1)
                dve.wait_ge(rinv_done, u + 1)
                dst = rows[:, bass.ds(b * TB, TB), g * HG * HD:(g + 1) * HG * HD].rearrange(
                    "p t (h w) -> p t h w", h=HG)
                nc.vector.tensor_tensor(dst, o4[:, :, :, 0:HD],
                                        rinv[:, :, :].unsqueeze(3).to_broadcast([P, TB, HG, HD]), ALU.mult
                                        ).then_inc(attn_rows, 1)

            dve.wait_ge(const_step, 3)
            for w in range(2):
                for p in range(8):
                    max_pair(w, p, w)
            for p in range(8):
                max_pair(2, p, 0)

            def dve_slot(u, bu, gu, s, more_max):
                for p in range(8):
                    if more_max:
                        max_pair(u + 2, p, s)
                    if p == 6:
                        normalise(u - 1, bu, gu)

            with dve.Fori(0, B - 1) as b:
                for r in range(1, NG + 1):
                    dve_slot(b * NG + r, b, r - 1, r % 2, True)
            dve_slot(UNITS - 3, B - 1, NG - 4, (UNITS - 3) % 2, True)

            def residual(t):
                if t == 1:
                    dve.wait_ge(resid_base, NT)
                if t >= 1:
                    dve.wait_ge(proj_ps, t)
                    nc.vector.scalar_tensor_tensor(x_sb[:, t - 1, :], projected(t - 1), tanh_g[:, 0:1],
                                                   x_sb[:, t - 1, :], ALU.mult, ALU.add).then_inc(x1_done, 1)
                if t < NT - TB:
                    dve.wait_ge(atT_ps, t + 1)
                    if t >= TB:
                        dve.wait_ge(proj_ps, t - TB + 1)
                    nc.vector.tensor_copy(attnT[:, t % TB, :, :], turned(t).rearrange("p (c n) -> p c n", c=DC)
                                          ).then_inc(atT_sb, 1)

            def stats2(b):
                dve.wait_ge(x1_done, (b + 1) * TB)
                ln_stats(b, B + b + 1)

            for i, u in enumerate((UNITS - 2, UNITS - 1)):
                for n, k in enumerate(PROJECT_AT):
                    if k > 11 and PROJECT_AT[n - 1] <= 11:
                        normalise(u - 1, (u - 1) // NG, (u - 1) % NG)
                    t = i * len(PROJECT_AT) + n
                    residual(t)
                    if t > TB and t % TB == 1:
                        stats2(t // TB - 1)
            normalise(UNITS - 1, B - 1, NG - 1)
            residual(NT - TB)
            stats2(2)
            ln_apply(0, B + 1)
            ln_apply(1, B + 2)
            for t in range(NT - TB + 1, NT + 1):
                residual(t)
            stats2(3)
            ln_apply(2, B + 3)
            ln_apply(3, B + 4)

            def shared_hidden(i, first, chunks=range(FC)):
                for f in chunks:
                    dve.wait_ge(sh_silu, FC * i + f + 1)
                    if not first:
                        dve.wait_ge(sh_y_ps, 2 * i)
                    nc.vector.tensor_tensor(sh_hT[:, f, :], sh_gate[:, f, :], bank(3 + f), ALU.mult
                                            ).then_inc(sh_hid, 1)

            def shared_added(i):
                for q in range(2):
                    dve.wait_ge(sh_y_ps, 2 * i + q + 1)
                    dst = x_sb[:, bass.ds(i * TB + 2 * q, 2), :]
                    nc.vector.scalar_tensor_tensor(dst, bank(6 + q).rearrange("p (t d) -> p t d", t=2),
                                                   tanh_g[:, 1:2], dst, ALU.mult, ALU.add).then_inc(sh_added, 1)

            r = [2]

            def step(ins):
                r[0] += 1
                ins.then_inc(route, 1)
                dve.wait_ge(route, r[0])

            dve.wait_ge(logit_ps, B)
            nc.vector.tensor_copy(logits[:, :, :], bank(7)[:, 0:NT * E].rearrange("p (t e) -> p t e", e=E)
                                  ).then_inc(chosen_done, 1)
            dve.wait_ge(chosen_done, 1)
            for t in range(NT):
                last = nc.vector.max(top8[:, t, :], logits[:, t, :])
            last.then_inc(chosen_done, 1)
            dve.wait_ge(chosen_done, 2)
            step(nc.vector.tensor_tensor(pexp[:, 0, :], top8[:, :, 1], top8[:, :, 0], ALU.subtract))
            for t in range(NT):
                last = nc.vector.max_index(top8_idx[:, t, :], top8[:, t, :], logits[:, t, :])
            step(last)
            step(nc.vector.tensor_copy(topi[:, :, :], top8_idx[:, :, 0:2].rearrange("p t k -> p k t")))
            for k in range(TOPK):
                last = nc.vector.tensor_tensor(onehot[:, k, :, :], topi[:, k, :].unsqueeze(2).to_broadcast([P, NT, E]),
                                               iota_e[:, :].unsqueeze(1).to_broadcast([P, NT, E]), ALU.is_equal)
            step(last)
            nc.vector.tensor_tensor(chosen[:, :, :], onehot[:, 0, :, :], onehot[:, 1, :, :], ALU.add
                                    ).then_inc(chosen_done, 1)
            dve.wait_ge(totals_ps, 1)
            nc.vector.tensor_copy(totals[:, :], bank(7)[:, 128:129].to_broadcast([P, P])).then_inc(totals_sb, 1)
            dve.wait_ge(pexp_done, 1)
            step(nc.vector.tensor_scalar(wsel[:, 1, :], pexp[:, 1, :], 1.0, None, ALU.add))
            step(nc.vector.reciprocal(wsel[:, 0, :], wsel[:, 1, :]))
            step(nc.vector.tensor_scalar(wsel[:, 0, :], wsel[:, 0, :], tanh_g[:, 1:2], None, ALU.mult))
            step(nc.vector.tensor_tensor(wsel[:, 1, :], wsel[:, 0, :], pexp[:, 1, :], ALU.mult))
            nc.vector.tensor_copy(slot_rows[:, :, TOKEN], token_f[:, :])
            nc.vector.tensor_copy(slot_rows[:, :, WEIGHT], wsel[:, 0, :]).then_inc(weight_set, 1)
            shared_hidden(0, True, range(1))
            dve.wait_ge(rank_ps, 1)
            nc.vector.tensor_copy(rank[:, :, :], bank(7)[:, 256:256 + NT * E].rearrange("p (t e) -> p t e", e=E))
            step(nc.vector.tensor_copy(count[:, :], bank(7)[:, 384:384 + E]))
            step(nc.vector.tensor_scalar(count_i[:, :], count[:, :], float(P - 1), None, ALU.add))
            step(nc.vector.tensor_scalar(blocks_i[:, :], count_i[:, :], 7, None, ALU.logical_shift_right))
            step(nc.vector.tensor_copy(blocks[:, :], blocks_i[:, :]))
            step(nc.vector.tensor_tensor_scan(ends[:, :], ones_bf[:, 0:E], blocks[:, :], 0.0, ALU.mult, ALU.add))
            step(nc.vector.tensor_tensor(base[:, :], ends[:, :], blocks[:, :], ALU.subtract))
            step(nc.vector.scalar_tensor_tensor(rank[:, :, :], base[:, :].unsqueeze(1).to_broadcast([P, NT, E]),
                                                float(P), rank[:, :, :], ALU.mult, ALU.add))
            step(nc.vector.tensor_tensor(onehot[:, :, :, :], onehot[:, :, :, :],
                                         rank[:, :, :].unsqueeze(1).to_broadcast([P, 2, NT, E]), ALU.mult))
            step(nc.vector.tensor_reduce(slot_f[:, :, :], onehot[:, :, :, :], AX.X, ALU.add))
            nc.vector.tensor_copy(slot_i[:, :, :], slot_f[:, :, :]).then_inc(slots_done, 1)
            step(nc.vector.tensor_tensor(past[:, :, :], ends[:, :].unsqueeze(1).to_broadcast([P, MAX_BLOCKS, E]),
                                         iota_b[:, :].unsqueeze(2).to_broadcast([P, MAX_BLOCKS, E]), ALU.is_le))
            step(nc.vector.tensor_reduce(block_e[:, :], past[:, :, :], AX.X, ALU.add))
            nc.vector.tensor_scalar(block_ei[:, :], block_e[:, :], float(E - 1), None, ALU.min).then_inc(slots_done, 1)
            shared_hidden(0, True, range(1, FC))
            shared_added(0)
            with dve.Fori(1, B - 1) as i:
                shared_hidden(i, False)
                shared_added(i)
            shared_hidden(B - 1, False)

            def at(j):
                return slice(j, j + 1) if isinstance(j, int) else bass.ds(j, 1)

            def copy_xT(j, s, first=False):
                dve.wait_ge(bxT_ps, j + 1)
                if not first:
                    dve.wait_ge(bup_ps, 2 * j - 2)
                nc.vector.tensor_copy(blk_xT[:, s, :, :], bank(4)[:, 0:D].rearrange("p (c n) -> p c n", c=DC)
                                      ).then_inc(bxT_sb, 1)
                nc.vector.tensor_copy(blk_row[:, at(j)], blk_x[:, s, TOKEN:TOKEN + 1])
                nc.vector.tensor_copy(blk_weight[:, at(j)], blk_x[:, s, WEIGHT:WEIGHT + 1]).then_inc(token_read, 1)

            def hidden(j, s, first=False):
                dve.wait_ge(bsilu, j + 1)
                dve.wait_ge(bup_ps, 2 * j + 2)
                if not first:
                    dve.wait_ge(bhT_ps, j)
                nc.vector.tensor_tensor(blk_h[:, :], blk_gate[:, :], bank(2 * s + 1)[:, 0:HALF], ALU.mult
                                        ).then_inc(bhid, 1)

            def copy_y(j, s, first=False):
                dve.wait_ge(by_ps, j + 1)
                if not first:
                    dve.wait_ge(by_out[s], ((j - s) // 2 if isinstance(j, int) else j_half[0]) * 16)
                dve.wait_ge(token_read, j + 1)
                nc.vector.tensor_scalar(blk_y[:, s, :], bank(6 + s)[:, 0:D], blk_weight[:, at(j)], None, ALU.mult
                                        ).then_inc(by_sb, 1)

            j_half = [None]
            copy_xT(0, 0, first=True)
            shared_added(B - 1)
            copy_xT(1, 1, first=True)
            hidden(0, 0, first=True)
            copy_xT(2, 0)
            hidden(1, 1)
            copy_y(0, 0, first=True)
            copy_xT(3, 1)
            hidden(2, 0)
            copy_y(1, 1, first=True)
            with dve.Fori(0, (MAX_BLOCKS - 5) // 2) as i:
                for q in range(2):
                    copy_xT(i * 2 + 4 + q, q)
                    hidden(i * 2 + 3 + q, (1 + q) % 2)
                    j_half[0] = i + 1
                    copy_y(i * 2 + 2 + q, q)
            for j in range(2 + 2 * ((MAX_BLOCKS - 5) // 2), MAX_BLOCKS):
                if j + 2 < MAX_BLOCKS:
                    copy_xT(j + 2, j % 2)
                if j + 1 < MAX_BLOCKS:
                    hidden(j + 1, (j + 1) % 2)
                copy_y(j, j % 2)

        @block.tensor
        def _(pe):
            def mm(o_, w, m, start=True, stop=True):
                return nc.tensor.matmul(o_, w, m, start=start, stop=stop)

            pe.wait_ge(ident_done, 1)

            def turn_xn(b):
                pe.wait_ge(rows_done, b + 1)
                if b >= 1:
                    pe.wait_ge(rowsT_sb, b)
                for t in range(TB):
                    for c in range(DC):
                        last = nc.tensor.transpose(bank(c)[:, t * P:(t + 1) * P],
                                                   rows[:, b * TB + t, c * P:(c + 1) * P], ident[:, :])
                last.then_inc(rowsT_ps, 1)

            def project_in(b, a, w_sb, first_bank, src, done):
                if b >= 1:
                    pe.wait_ge(resid_done, QK_ORDER.index((a, b - 1)) + 1)
                for c in range(DC):
                    for d in range(DC):
                        last = mm(bank(first_bank + c), w_sb[:, d, c * P:(c + 1) * P], src[:, d, b * T:(b + 1) * T],
                                  d == 0, d == DC - 1)
                last.then_inc(done, 1)

            def project_v(b):
                if b >= 1:
                    pe.wait_ge(v_done, b)
                for kt in range(TB):
                    for d in range(DC):
                        tok = b * T + kt * P
                        last = mm(bank(6 + kt // 2)[:, (kt % 2) * D:(kt % 2 + 1) * D], ctx_sb[:, d, tok:tok + P],
                                  wkv_sb[:, d, D:2 * D], d == 0, d == DC - 1)
                last.then_inc(v_ps, 1)

            turn_xn(0)
            for b in range(B):
                if b == 0:
                    pe.wait_ge(wq_in, 16)
                pe.wait_ge(rowsT_sb, b + 1)
                project_in(b, 0, wq_sb, 2, xnT, q_ps)
                if b == 0:
                    pe.wait_ge(wkv_in, 16)
                pe.wait_ge(ctx_in[b], 16)
                project_in(b, 1, wkv_sb, 4, ctx_sb, k_ps)
                if b + 1 < B:
                    turn_xn(b + 1)
                project_v(b)

            def max_tile(w, i, s, waits):
                p = i // 2
                if i % 2 == 0 and waits(p):
                    pe.wait_ge(max_done, 8 * w + p - 1)
                h, qt = i // TB, i % TB
                last = mm(bank(2 * (p % 2) + i % 2), q_unit[0:KROWS, s, h, qt * P:(qt + 1) * P],
                          k_unit[0:KROWS, s, h, :])
                if i % 2 == 1:
                    last.then_inc(pair_ps, 1)

            def turn_max(w, s):
                pe.wait_ge(max_done, 8 * w + 8)
                nc.tensor.transpose(bank(7)[:, 0:P], neg_max[:, s, :], ident[:, :]).then_inc(nmT_ps, 1)

            def pv(u, s, kt, half, first=False):
                if half == 0:
                    pe.wait_ge(exp_done, u * TB * HG + kt * HG + HG)
                    if kt == 0 and not first:
                        pe.wait_ge(o_done, u)
                cols = slice(half * T // 2, (half + 1) * T // 2)
                for h in range(HG):
                    last = nc.tensor.matmul(bank(6)[h * VW:(h + 1) * VW, cols], v_unit[:, s, kt, h * VW:(h + 1) * VW],
                                            probs[:, (kt * HG + h) % 8, cols], start=kt == 0 and half == 0,
                                            stop=kt == TB - 1, skip_group_check=True)
                if half == 1:
                    last.then_inc(pv_done, 1)

            def turn_out(u, s, qt):
                if qt == 0:
                    pe.wait_ge(o_done, u + 1)
                last = nc.tensor.transpose(bank(7)[:, qt * P:(qt + 1) * P], o_sb[:, s, qt * P:(qt + 1) * P], ident[:, :])
                if qt == TB - 1:
                    last.then_inc(oT_ps, 1)

            def slot(u, bu, r, first=False, more_max=True, more_turn=True, also=lambda k: None):
                s, w = r % NG, (r + 2) % NG
                if more_max:
                    pe.wait_ge(unit_in[w], 16 * LOADS * (bu + (r + 2) // NG + 1))
                pe.wait_ge(nm_in[s], 16 * MROWS * (bu + r // NG + 1))
                for k in range(TB * HG):
                    kt, h = k // HG, k % HG
                    if not (first and k < 2):
                        pe.wait_ge(exp_done, u * TB * HG + k - 1)
                    mm(bank(4 + k % 2), k_unit[0:KROWS + MROWS, s, h, kt * P:(kt + 1) * P],
                       q_unit[0:KROWS + MROWS, s, h, :]).then_inc(score_ps, 1)
                    if more_max:
                        max_tile(u + 2, k, w, lambda p: True)
                    if k in (2, 3) and not first:
                        pv(u - 1, (r - 1) % NG, TB - 1, k - 2)
                    if k == TURN_MAX and more_turn:
                        if first:
                            pe.wait_ge(nmT_sb, 1)
                        else:
                            pe.wait_ge(attn_rows, u)
                        turn_max(u + 1, (r + 1) % 2)
                    if k in TURN_OUT and not first:
                        if k == TURN_OUT[0]:
                            if more_turn:
                                pe.wait_ge(nmT_sb, u + 2)
                            else:
                                pe.wait_ge(attn_rows, u)
                        turn_out(u - 1, (r - 1) % 2, k - TURN_OUT[0])
                    if kt >= 1 and k % 2 == 1:
                        pv(u, s, kt - 1, k % HG // 2, first)
                    also(k)

            TURN_MAX, TURN_OUT = 1, (8, 9, 10, 11)

            pe.wait_ge(ones_rows, 1)
            pe.wait_ge(const_step, 3)
            pe.wait_ge(rowsT_sb, B)
            pe.wait_ge(resid_done, 2 * B - 1)
            for w in range(2):
                pe.wait_ge(unit_in[w], 16 * LOADS)
                for i in range(16):
                    max_tile(w, i, w, lambda p, w=w: w > 0 or p >= 2)
                if w == 0:
                    pe.wait_ge(v_done, B)
                    turn_max(0, 0)
            pe.wait_ge(resid_done, 2 * B)
            slot(0, 0, 0, first=True)
            with pe.Fori(0, B - 1) as b:
                for r in range(1, NG + 1):
                    slot(b * NG + r, b, r)

            def turn_attn(t):
                for c in range(DC):
                    last = nc.tensor.transpose(turned(t)[:, c * P:(c + 1) * P], rows[:, t, c * P:(c + 1) * P],
                                               ident[:, :])
                last.then_inc(atT_ps, 1)

            def project(t):
                pe.wait_ge(atT_sb, t + 1)
                for c in range(DC):
                    last = mm(projected(t), attnT[:, t % TB, c, :], wp_sb[:, c, :], c == 0, c == DC - 1)
                last.then_inc(proj_ps, 1)

            def project_out(t):
                if t >= 1:
                    if t >= 3:
                        pe.wait_ge(x1_done, t - 2)
                    project(t - 1)
                if t < NT - TB:
                    turn_attn(t)

            slot(UNITS - 3, B - 1, NG - 3)
            pe.wait_ge(small_in, 16 * 3)
            pe.wait_ge(max_done, 8 * UNITS)
            pe.wait_ge(attn_rows, (B - 1) * NG + 1)
            for u in (UNITS - 2, UNITS - 1):
                base_t = (u - UNITS + 2) * len(PROJECT_AT)
                slot(u, B - 1, u % NG, more_max=False, more_turn=u + 1 < UNITS,
                     also=lambda k: project_out(base_t + PROJECT_AT.index(k)) if k in PROJECT_AT else None)
            for half in range(2):
                pv(UNITS - 1, (UNITS - 1) % NG, TB - 1, half)
            pe.wait_ge(attn_rows, UNITS)
            for qt in range(TB):
                turn_out(UNITS - 1, (UNITS - 1) % 2, qt)
            project_out(NT - TB)

            def turn_rows(b):
                pe.wait_ge(rows_done, B + b + 1)
                if b >= 2:
                    pe.wait_ge(rowsT_sb, B + b - 1)
                elif b == 1:
                    pe.wait_ge(x1_done, NT - TB + 1)
                else:
                    pe.wait_ge(atT_sb, NT)
                for t in range(TB):
                    for c in range(DC):
                        last = nc.tensor.transpose(rowsT_bank(b, c)[:, t * P:(t + 1) * P],
                                                   rows[:, b * TB + t, c * P:(c + 1) * P], ident[:, :])
                last.then_inc(rowsT_ps, 1)

            def router(b):
                pe.wait_ge(rowsT_sb, B + b + 1)
                for t in range(b * TB, (b + 1) * TB):
                    for c in range(DC):
                        last = mm(bank(7)[:, t * E:(t + 1) * E], xnT[:, c, t * P:(t + 1) * P], gate_sb[:, c, :],
                                  c == 0, c == DC - 1)
                last.then_inc(logit_ps, 1)

            def shared_up(i, f, first):
                if not first:
                    pe.wait_ge(sh_hid, FC * i + f - FC + 1)
                for half in range(2):
                    for c in range(DC):
                        col = half * HALF + f * P
                        last = mm(bank(3 * half + f), w_up[:, E, c, col:col + P], xnT[:, c, bass.ds(i * T, T)],
                                  c == 0, c == DC - 1)
                last.then_inc(sh_up_ps, 1)

            def shared_down(i, first):
                pe.wait_ge(sh_hid, FC * i + FC)
                for q in range(2):
                    if not first:
                        pe.wait_ge(sh_added, 2 * i + q - 1)
                    for t in range(2):
                        for f in range(FC):
                            tok = (2 * q + t) * P
                            last = mm(bank(6 + q)[:, t * D:(t + 1) * D], sh_hT[:, f, tok:tok + P], w_dn[:, E, f, :],
                                      f == 0, f == FC - 1)
                    last.then_inc(sh_y_ps, 1)

            pe.wait_ge(attn_rows, UNITS + 1)
            for t in range(NT - TB, NT):
                turn_attn(t)
            for t in range(NT - TB, NT):
                if t == NT - TB + 1:
                    pe.wait_ge(x1_done, NT - TB)
                project(t)
            for b in range(2):
                turn_rows(b)
            for b in range(2):
                router(b)
            for b in range(2, B):
                turn_rows(b)
            for b in range(2, B):
                router(b)
            pe.wait_ge(w_ffn_in, 16 * 2 * (E + 1))
            pe.wait_ge(x1_done, NT)
            shared_up(0, 0, True)
            pe.wait_ge(chosen_done, 3)
            mm(bank(7)[:, 128:129], chosen[:, :, :].rearrange("p t e -> p (t e)"), ones_bf[:, 0:1]).then_inc(totals_ps, 1)
            shared_up(0, 1, True)
            pe.wait_ge(totals_sb, 1)
            pe.wait_ge(const_step, 10)
            mm(bank(7)[:, 256:256 + NT * E], before[:, :], chosen[:, :, :].rearrange("p t e -> p (t e)"), True, False)
            mm(bank(7)[:, 256:256 + NT * E], totals[:, :], before_tile[:, :, :].rearrange("p t e -> p (t e)"),
               False, True)
            mm(bank(7)[:, 384:384 + E], totals[:, :], same_e_bf[:, :]).then_inc(rank_ps, 1)
            shared_up(0, 2, True)
            shared_up(1, 0, False)
            shared_down(0, True)
            shared_up(1, 1, False)
            shared_up(1, 2, False)
            with pe.Fori(2, B) as i:
                shared_up(i, 0, False)
                shared_down(i - 1, False)
                shared_up(i, 1, False)
                shared_up(i, 2, False)

            def expert(j):
                return pe.value_load(block_ei[0:1, bass.ds(j, 1)], min_val=0, max_val=E - 1)

            def turn_x(j, s, half, first=False):
                pe.wait_ge(bx_in[s], 16 * (half + 1))
                if not first:
                    pe.wait_ge(bxT_sb, j)
                for c in range(DC):
                    last = nc.tensor.transpose(bank(4)[:, c * P:(c + 1) * P], blk_x[:, s, c * P:(c + 1) * P],
                                               ident[:, :])
                last.then_inc(bxT_ps, 1)

            def up(j, s, first=False):
                e = expert(j)
                pe.wait_ge(bxT_sb, j + 1)
                if not first:
                    pe.wait_ge(bhid, j - 1)
                for g in range(2):
                    for c in range(DC):
                        last = mm(bank(2 * s + g)[:, 0:HALF], blk_xT[:, s, c, :],
                                  w_up[:, bass.ds(e, 1), c, g * HALF:(g + 1) * HALF].rearrange("p a f -> p (a f)"),
                                  c == 0, c == DC - 1)
                    last.then_inc(bup_ps, 1)

            def turn_h(j, first=False):
                pe.wait_ge(bhid, j + 1)
                if not first:
                    pe.wait_ge(bhT_sb, j)
                for f in range(FC):
                    last = nc.tensor.transpose(bank(5)[:, f * P:(f + 1) * P], blk_h[:, f * P:(f + 1) * P], ident[:, :])
                last.then_inc(bhT_ps, 1)

            def down(j, s, first=False):
                e = expert(j)
                pe.wait_ge(bhT_sb, j + 1)
                if first:
                    pe.wait_ge(sh_added, 2 * B)
                else:
                    pe.wait_ge(by_sb, j - 1)
                for f in range(FC):
                    last = mm(bank(6 + s)[:, 0:D], blk_hT[:, f, :],
                              w_dn[:, bass.ds(e, 1), f, :].rearrange("p a n -> p (a n)"), f == 0, f == FC - 1)
                last.then_inc(by_ps, 1)

            pe.wait_ge(slots_done, 2)
            pe.wait_ge(sh_hid, FC * B - 1)
            turn_x(0, 0, 0, first=True)
            shared_down(B - 1, False)
            turn_x(1, 1, 0)
            up(0, 0, first=True)
            turn_h(0, first=True)
            turn_x(2, 0, 1)
            up(1, 1, first=True)
            down(0, 0, first=True)
            turn_h(1)
            turn_x(3, 1, 1)
            up(2, 0)
            down(1, 1, first=True)
            with pe.Fori(0, (MAX_BLOCKS - 5) // 2) as i:
                for q in range(2):
                    turn_h(i * 2 + 2 + q)
                    turn_x(i * 2 + 4 + q, q, i + 2)
                    up(i * 2 + 3 + q, (1 + q) % 2)
                    down(i * 2 + 2 + q, q)
            for j in range(2 + 2 * ((MAX_BLOCKS - 5) // 2), MAX_BLOCKS):
                turn_h(j)
                if j + 2 < MAX_BLOCKS:
                    turn_x(j + 2, j % 2, (j + 2) // 2)
                if j + 1 < MAX_BLOCKS:
                    up(j + 1, (j + 1) % 2)
                down(j, j % 2)


def kernel(x, ctx_1024, g_xattn, g_ffn, L0_xattn_W_kv, L0_xattn_W_q, L0_xattn_W_proj, L0_xattn_b_proj,
           L0_ffn_gate_w, L0_ffn_w_up, L0_ffn_w_down, L0_ffn_sg_gate, L0_ffn_sg_up, L0_ffn_sg_down):
    import concourse.bacc as bacc
    from concourse.bass_utils import run_bass_kernel_spmd

    def arr(a):
        return np.asarray(a)

    def by_unit(w):
        return w.reshape(D, NG, HG, HD).transpose(0, 1, 3, 2).reshape(D, D)

    shared_up = np.concatenate([arr(L0_ffn_sg_gate), arr(L0_ffn_sg_up)], axis=0)[None]
    host = {
        "x": arr(x),
        "ctxT": arr(ctx_1024).reshape(N, D).T,
        "g_xattn": arr(g_xattn),
        "g_ffn": arr(g_ffn),
        "w_kv": np.concatenate([by_unit(arr(L0_xattn_W_kv)[:, :D]), arr(L0_xattn_W_kv)[:, D:]], axis=1),
        "w_q": by_unit(arr(L0_xattn_W_q)),
        "w_proj": arr(L0_xattn_W_proj),
        "b_proj": arr(L0_xattn_b_proj),
        "gateT": arr(L0_ffn_gate_w).T,
        "w_upT": np.concatenate([arr(L0_ffn_w_up), shared_up], axis=0).transpose(0, 2, 1),
        "w_downT": np.concatenate([arr(L0_ffn_w_down), arr(L0_ffn_sg_down)[None]], axis=0).transpose(0, 2, 1),
    }
    host = {k: np.ascontiguousarray(v) for k, v in host.items()}
    nc = bacc.Bacc("TRN2", target_bir_lowering=False, num_devices=1)
    args = [nc.dram_tensor(f"in_{k}", v.shape, mybir.dt.from_np(v.dtype), kind="ExternalInput").ap()
            for k, v in host.items()]
    out = nc.dram_tensor("out", (OUT_ROWS, D), F32, kind="ExternalOutput").ap()
    build(nc, *args, out)
    r = run_bass_kernel_spmd(nc, [{f"in_{k}": v for k, v in host.items()}], core_ids=[0])
    return r.results[0]["out"][0:N].reshape(B, T, D)
```
